# Optimizing a Trainium2 kernel written in Bass

```python
import numpy as np
import jax
import jax.numpy as jnp

def _softmax(x, axis=-1):
    return jax.nn.softmax(x, axis=axis)

def _gelu(x):
    return jax.nn.gelu(x, approximate=True)

def _silu(x):
    return jax.nn.silu(x)

def _sigmoid(x):
    return jax.nn.sigmoid(x)

def _layernorm(x, axis=-1, eps=1e-05):
    m = jnp.mean(x, axis=axis, keepdims=True)
    v = jnp.var(x, axis=axis, keepdims=True)
    return (x - m) / jnp.sqrt(v + eps)

def _scatter_add(tgt, idx, src, axis=0):
    return tgt.at[idx].add(src)

def _segment_sum(src, seg, n):
    return jax.ops.segment_sum(src, seg, n)
kernel_name = 'mk_adaln_d1_jaxref_r2_789f65'

def setup_inputs(seed: int=0):
    np.random.seed(seed)
    _w = jnp.asarray

    def _L0_attn_setup():
        import jax, jax.numpy as jnp
        import numpy as np
        B, L = (2, 512)
        D_MODEL = 512
        D_STATE = 16
        K = 3
        EXPAND = 1
        D_INNER = D_MODEL * EXPAND

        def _silu(v):
            return v * jax.nn.sigmoid(v)

        def _mamba_fwd(x, W_in, conv_w, W_B, W_C, W_delta, delta_base, W_tau, A_log, W_out):
            residual = x
            z = x @ W_in
            val, gate = jnp.split(z, 2, axis=-1)
            v = jnp.transpose(val, (0, 2, 1))
            v = jax.lax.conv_general_dilated(v, conv_w, window_strides=(1,), padding=[((K - 1) // 2, (K - 1) // 2)], dimension_numbers=('NCH', 'OIH', 'NCH'), feature_group_count=D_INNER)
            val = jnp.transpose(_silu(v), (0, 2, 1))
            B_proj = val @ W_B
            C_proj = val @ W_C
            combined_delta = val @ W_delta + delta_base
            Delta = jax.nn.softplus(combined_delta @ W_tau)
            A = -jnp.exp(A_log)
            dA = Delta[..., None] * A
            A_bar = jnp.exp(dA)
            B_bar = jnp.expm1(dA) / (dA + 1e-06) * Delta[..., None] * B_proj[:, :, None, :]

            def step(h, inp):
                a_t, b_t, c_t, u_t = inp
                h = a_t * h + b_t * u_t[..., None]
                y_t = jnp.sum(h * c_t[:, None, :], axis=-1)
                return (h, y_t)
            h0 = jnp.zeros((x.shape[0], D_INNER, D_STATE), dtype=x.dtype)
            xs = (jnp.moveaxis(A_bar, 1, 0), jnp.moveaxis(B_bar, 1, 0), jnp.moveaxis(C_proj, 1, 0), jnp.moveaxis(val, 1, 0))
            _, ys = jax.lax.scan(step, h0, xs)
            y = jnp.moveaxis(ys, 0, 1)
            out = y * _silu(gate) @ W_out + residual
            return out
        key = jax.random.key(seed)
        ks = jax.random.split(key, 10)
        s = 0.02
        x = jax.random.normal(ks[0], (B, L, D_MODEL), dtype=jnp.float32)
        W_in = jax.random.normal(ks[1], (D_MODEL, 2 * D_INNER), dtype=jnp.float32) * s
        conv_w = jax.random.normal(ks[2], (D_INNER, 1, K), dtype=jnp.float32) * s
        W_B = jax.random.normal(ks[3], (D_INNER, D_STATE), dtype=jnp.float32) * s
        W_C = jax.random.normal(ks[4], (D_INNER, D_STATE), dtype=jnp.float32) * s
        W_delta = jax.random.normal(ks[5], (D_INNER, D_MODEL), dtype=jnp.float32) * s
        delta_base = jax.random.normal(ks[6], (D_MODEL,), dtype=jnp.float32)
        W_tau = jax.random.normal(ks[7], (D_MODEL, D_MODEL), dtype=jnp.float32) * s
        A_log = jnp.tile(jnp.log(jnp.arange(1, D_STATE + 1, dtype=jnp.float32)), (D_MODEL, 1))
        W_out = jax.random.normal(ks[8], (D_INNER, D_MODEL), dtype=jnp.float32) * s
        return {'x': x, 'W_in': W_in, 'conv_w': conv_w, 'W_B': W_B, 'W_C': W_C, 'W_delta': W_delta, 'delta_base': delta_base, 'W_tau': W_tau, 'A_log': A_log, 'W_out': W_out}
    _L0_attn_in = _L0_attn_setup()

    def _L0_ffn_setup():
        import jax, jax.numpy as jnp
        import numpy as np
        B, S, D, E, H, K = (4, 1024, 512, 8, 256, 2)
        key = jax.random.key(seed)
        ks = jax.random.split(key, 11)
        sc = 0.02
        return {'x': jax.random.normal(ks[0], (B, S, D), dtype=jnp.float32), 'gate_W': jax.random.normal(ks[1], (D, E), dtype=jnp.float32) * sc, 'W1': jax.random.normal(ks[2], (E, D, H), dtype=jnp.float32) * sc, 'b1': jnp.zeros((E, H), dtype=jnp.float32), 'W2': jax.random.normal(ks[3], (E, H, D), dtype=jnp.float32) * sc, 'b2': jnp.zeros((E, D), dtype=jnp.float32), 'Ws1': jax.random.normal(ks[4], (D, H), dtype=jnp.float32) * sc, 'bs1': jnp.zeros((H,), dtype=jnp.float32), 'Ws2': jax.random.normal(ks[5], (H, D), dtype=jnp.float32) * sc, 'bs2': jnp.zeros((D,), dtype=jnp.float32), 'route_scale': jnp.ones((), dtype=jnp.float32)}
    _L0_ffn_in = _L0_ffn_setup()
    _L0_c = _w((lambda *s: np.random.randn(*s).astype(np.float32) * 0.05)(4, 512))
    _L0_wmod = _w((lambda *s: np.random.randn(*s).astype(np.float32) * 0.05)(512, 6 * 512) * 512 ** (-0.5))
    _d = {'L0_attn_x': _L0_attn_in['x'], 'L0_attn_W_in': _L0_attn_in['W_in'], 'L0_attn_conv_w': _L0_attn_in['conv_w'], 'L0_attn_W_B': _L0_attn_in['W_B'], 'L0_attn_W_C': _L0_attn_in['W_C'], 'L0_attn_W_delta': _L0_attn_in['W_delta'], 'L0_attn_delta_base': _L0_attn_in['delta_base'], 'L0_attn_W_tau': _L0_attn_in['W_tau'], 'L0_attn_A_log': _L0_attn_in['A_log'], 'L0_attn_W_out': _L0_attn_in['W_out'], 'L0_ffn_gate_W': _L0_ffn_in['gate_W'], 'L0_ffn_W1': _L0_ffn_in['W1'], 'L0_ffn_b1': _L0_ffn_in['b1'], 'L0_ffn_W2': _L0_ffn_in['W2'], 'L0_ffn_b2': _L0_ffn_in['b2'], 'L0_ffn_Ws1': _L0_ffn_in['Ws1'], 'L0_ffn_bs1': _L0_ffn_in['bs1'], 'L0_ffn_Ws2': _L0_ffn_in['Ws2'], 'L0_ffn_bs2': _L0_ffn_in['bs2'], 'L0_ffn_route_scale': _L0_ffn_in['route_scale'], 'L0_c': _L0_c, 'L0_wmod': _L0_wmod}
    _x0 = _d['L0_attn_x']
    _d['L0_attn_x'] = jax.random.normal(jax.random.fold_in(jax.random.key(seed), 1), (4, 2048, 512), dtype=_x0.dtype)
    del _x0
    return _d

def reference(L0_attn_x, L0_attn_W_in, L0_attn_conv_w, L0_attn_W_B, L0_attn_W_C, L0_attn_W_delta, L0_attn_delta_base, L0_attn_W_tau, L0_attn_A_log, L0_attn_W_out, L0_ffn_gate_W, L0_ffn_W1, L0_ffn_b1, L0_ffn_W2, L0_ffn_b2, L0_ffn_Ws1, L0_ffn_bs1, L0_ffn_Ws2, L0_ffn_bs2, L0_ffn_route_scale, L0_c, L0_wmod):

    def _L0_attn_ref(x, W_in, conv_w, W_B, W_C, W_delta, delta_base, W_tau, A_log, W_out):
        import jax, jax.numpy as jnp
        import numpy as np
        B, L = (2, 512)
        D_MODEL = 512
        D_STATE = 16
        K = 3
        EXPAND = 1
        D_INNER = D_MODEL * EXPAND

        def _silu(v):
            return v * jax.nn.sigmoid(v)

        def _mamba_fwd(x, W_in, conv_w, W_B, W_C, W_delta, delta_base, W_tau, A_log, W_out):
            residual = x
            z = x @ W_in
            val, gate = jnp.split(z, 2, axis=-1)
            v = jnp.transpose(val, (0, 2, 1))
            v = jax.lax.conv_general_dilated(v, conv_w, window_strides=(1,), padding=[((K - 1) // 2, (K - 1) // 2)], dimension_numbers=('NCH', 'OIH', 'NCH'), feature_group_count=D_INNER)
            val = jnp.transpose(_silu(v), (0, 2, 1))
            B_proj = val @ W_B
            C_proj = val @ W_C
            combined_delta = val @ W_delta + delta_base
            Delta = jax.nn.softplus(combined_delta @ W_tau)
            A = -jnp.exp(A_log)
            dA = Delta[..., None] * A
            A_bar = jnp.exp(dA)
            B_bar = jnp.expm1(dA) / (dA + 1e-06) * Delta[..., None] * B_proj[:, :, None, :]

            def step(h, inp):
                a_t, b_t, c_t, u_t = inp
                h = a_t * h + b_t * u_t[..., None]
                y_t = jnp.sum(h * c_t[:, None, :], axis=-1)
                return (h, y_t)
            h0 = jnp.zeros((x.shape[0], D_INNER, D_STATE), dtype=x.dtype)
            xs = (jnp.moveaxis(A_bar, 1, 0), jnp.moveaxis(B_bar, 1, 0), jnp.moveaxis(C_proj, 1, 0), jnp.moveaxis(val, 1, 0))
            _, ys = jax.lax.scan(step, h0, xs)
            y = jnp.moveaxis(ys, 0, 1)
            out = y * _silu(gate) @ W_out + residual
            return out
        return _mamba_fwd(x, W_in, conv_w, W_B, W_C, W_delta, delta_base, W_tau, A_log, W_out)

    def _L0_ffn_ref(x, gate_W, W1, b1, W2, b2, Ws1, bs1, Ws2, bs2, route_scale):
        import jax, jax.numpy as jnp
        import numpy as np
        B, S, D, E, H, K = (4, 1024, 512, 8, 256, 2)
        scores = jax.nn.sigmoid(x @ gate_W) * route_scale
        topk_scores, topk_idx = jax.lax.top_k(scores, K)
        topk_w = topk_scores / topk_scores.sum(-1, keepdims=True)
        onehot = jax.nn.one_hot(topk_idx, E, dtype=x.dtype)
        gate_full = jnp.einsum('bsk,bske->bse', topk_w, onehot)
        h = jax.nn.gelu(jnp.einsum('bsd,edh->bseh', x, W1) + b1, approximate=False)
        y = jnp.einsum('bseh,ehd->bsed', h, W2) + b2
        expert_out = jnp.einsum('bse,bsed->bsd', gate_full, y)
        shared = jax.nn.gelu(x @ Ws1 + bs1, approximate=False) @ Ws2 + bs2
        return expert_out + shared
    x = L0_attn_x
    mod = (_silu(L0_c) @ L0_wmod).reshape(L0_c.shape[0], 6, 1, -1)
    sa, ca, ga, sb, cb, gb = (mod[:, 0], mod[:, 1], mod[:, 2], mod[:, 3], mod[:, 4], mod[:, 5])
    ga = (2 * (ga >= 0) - 1) * jnp.maximum(jnp.abs(ga), 0.25)
    gb = (2 * (gb >= 0) - 1) * jnp.maximum(jnp.abs(gb), 0.25)
    h = _layernorm(x, axis=-1) * (1 + ca) + sa
    x = x + ga * _L0_attn_ref(h, L0_attn_W_in, L0_attn_conv_w, L0_attn_W_B, L0_attn_W_C, L0_attn_W_delta, L0_attn_delta_base, L0_attn_W_tau, L0_attn_A_log, L0_attn_W_out)
    h = _layernorm(x, axis=-1) * (1 + cb) + sb
    x = x + gb * _L0_ffn_ref(h, L0_ffn_gate_W, L0_ffn_W1, L0_ffn_b1, L0_ffn_W2, L0_ffn_b2, L0_ffn_Ws1, L0_ffn_bs1, L0_ffn_Ws2, L0_ffn_bs2, L0_ffn_route_scale)
    return x

_drawn_inputs = setup_inputs


def setup_inputs(seed=0):
    import zlib

    import numpy as np

    out = dict(_drawn_inputs(seed))
    spreads = {'L0_ffn_b1': (0.0, 2.0),
     'L0_ffn_b2': (0.0, 2.0),
     'L0_ffn_bs1': (0.0, 2.0),
     'L0_ffn_bs2': (0.0, 1.872)}
    factors = {'L0_attn_W_in': 8.0,
     'L0_attn_conv_w': 8.0,
     'L0_attn_W_B': 8.0,
     'L0_attn_W_C': 8.0,
     'L0_attn_delta_base': 8.0,
     'L0_attn_W_tau': 8.0,
     'L0_attn_A_log': 8.0,
     'L0_attn_W_out': 8.0,
     'L0_ffn_gate_W': 2.915,
     'L0_ffn_W1': 4.164,
     'L0_ffn_W2': 3.9,
     'L0_ffn_Ws1': 2.956,
     'L0_ffn_Ws2': 2.762}
    for name, (base, spread) in spreads.items():
        noise = np.random.default_rng([zlib.crc32(name.encode()), seed]).standard_normal(out[name].shape)
        drawn = base * np.exp(spread * noise) if base else spread * noise
        out[name] = jnp.asarray(drawn.astype(out[name].dtype))
    for name, factor in factors.items():
        out[name] = (out[name] * factor).astype(out[name].dtype)
    return out
```

```python
from contextlib import ExitStack

import numpy as np
import concourse.bass as bass
from concourse import mybir

ALU = mybir.AluOpType
ACT = mybir.ActivationFunctionType
F32 = mybir.dt.float32
BF16 = mybir.dt.bfloat16
AX_X = mybir.AxisListType.X

P = 128
BANK = 512
LN_EPS = 1e-5
DA_EPS = float(np.float32(1e-6))
Z_CAP = 4e9


def adaln_mamba_moe(nc, x, W_in, conv_w, W_BC, W_deltaT, delta_base, W_tau, A_log, W_out, gate_W, W1, b1, W2, b2,
                    route_scale, cT, wmod, ident, onehot, earlier, out):
    NB, L, D = x.shape
    G = D // P
    N = A_log.shape[1]
    TT = L // P
    TB = L // BANK
    NE = W1.shape[1] // D
    E = gate_W.shape[1]
    EX = E + 1
    HID = W1.shape[1] // EX
    HT = HID // P
    MODS = wmod.shape[1] // D
    J = 2
    NK = N // J
    HALF = L // 2
    TPB = BANK // P
    NBLK = NB * L // BANK

    h_gate = nc.dram_tensor("gate_scratch", [G, P, L], F32).ap()
    h_x1 = nc.dram_tensor("x1_scratch", [NB * L, D], F32).ap()
    h_mod = nc.dram_tensor("mod_scratch", [NB, MODS * D], F32).ap()
    h_wdt = nc.dram_tensor("w_delta_tau_scratch", [P, G * D], F32).ap()

    with ExitStack() as ctx:
        ctx.enter_context(nc.allow_non_contiguous_dma(reason="small per-channel tables"))

        def sb(name, shape, dt=F32):
            return ctx.enter_context(nc.sbuf_tensor(name, shape, dt))

        def sem(name):
            return ctx.enter_context(nc.semaphore(name))

        ps = ctx.enter_context(nc.psum_tensor("ps", [P, 8, BANK], F32))

        identity = sb("identity", [P, P])
        pick = sb("pick", [3 * 2 * N, 2 * N * P], BF16)
        conv_taps = sb("conv_taps", [P, G, 3])
        negA = sb("negA", [P, G * N])
        halfA = sb("halfA", [P, G * N])
        z_scale = sb("z_scale", [P, G * N])
        recipA = sb("recipA", [P, G * N])
        tau_bias = sb("tau_bias", [P, G])
        modT = sb("modT", [P, MODS, G])
        consts = sb("consts", [P, 3])
        moments = sb("moments", [P, TT, 2])
        spread = sb("spread", [P, TT])
        rstd = sb("rstd", [P, TT])
        stats = sb("stats", [P, TT, 6])
        u = sb("u", [P, G, L])
        delta = sb("delta", [P, G, L])
        BC3 = sb("BC3", [3 * 2 * N, L], BF16)
        split = sb("split", [2 * N, 2, BANK])
        mid16 = sb("mid16", [2 * N, BANK], BF16)
        WORK = 30880
        work = sb("work", [P, WORK])

        class Carve:
            def __init__(self):
                self.at = 0

            def __call__(self, words):
                a = self.at
                self.at += words
                assert self.at <= WORK, self.at
                return work[:, a:a + words]

        c = Carve()
        wmod_sb = c(G * MODS * D).rearrange("p (k n) -> p k n", k=G)
        wdT = c(G * D).rearrange("p (k n) -> p k n", k=G)
        wtau = c(G * D).rearrange("p (k n) -> p k n", k=G)
        wdt_out = c(G * D).rearrange("p (k n) -> p k n", k=G)
        cs = c(G * NB).rearrange("p (k b) -> p k b", k=G)
        csilu = c(G * NB).rearrange("p (k b) -> p k b", k=G)
        base = c(G)
        alog = c(G * N)
        absA = c(G * N)
        rows = c(MODS * D).rearrange("p (m d) -> p m d", m=MODS)
        signs = c(2 * D).rearrange("p (m d) -> p m d", m=2)
        mags = c(2 * D).rearrange("p (m d) -> p m d", m=2)

        x1_st = sem("work_space_stored")
        ld = sem("setup_loads")
        silu_done, a_done, mod_mm, wdt_mm, setup_v, wdt_ev, setup_st = (
            sem("silu_done"), sem("a_done"), sem("mod_mm"), sem("wdt_mm"), sem("setup_vector"), sem("wdt_evicted"),
            sem("setup_stores"))
        with nc.Block() as block:
            @block.sync
            def _(sp):
                kp = "(k p) n -> p k n"
                sp.dma_start(cs, cT.rearrange(kp, p=P)).then_inc(ld, 16)
                sp.dma_start(wmod_sb, wmod.rearrange(kp, p=P)).then_inc(ld, 16)
                sp.dma_start(wdT, W_deltaT.rearrange(kp, p=P)).then_inc(ld, 16)
                sp.dma_start(wtau, W_tau.rearrange(kp, p=P)).then_inc(ld, 16)
                sp.dma_start(base, delta_base.rearrange("(k p) -> p k", p=P)).then_inc(ld, 16)
                sp.dma_start(alog.rearrange("p (g n) -> p g n", g=G), A_log.rearrange("(g p) n -> p g n", p=P)).then_inc(ld, 16)
                sp.dma_start(conv_taps[:], conv_w.rearrange("(g p) n -> p g n", p=P)).then_inc(ld, 16)
                sp.dma_start(identity[:], ident).then_inc(ld, 16)
                sp.dma_start(pick[:], onehot).then_inc(ld, 16)
                sp.wait_ge(setup_v, 16)
                sp.dma_start(h_mod.rearrange("b (m d) -> b m d", m=MODS), rows[0:NB]).then_inc(setup_st, 16)
                sp.wait_ge(wdt_ev, G)
                sp.dma_start(h_wdt.rearrange("p (k n) -> p k n", k=G), wdt_out).then_inc(x1_st, 16)
                sp.wait_ge(setup_st, 16)
                sp.wait_ge(x1_st, 16)

            @block.scalar
            def _(act):
                act.wait_ge(ld, 16 * 9)
                nc.scalar.activation(csilu, cs, ACT.Silu).then_inc(silu_done, 1)
                nc.scalar.activation(absA, alog, ACT.Exp).then_inc(a_done, 1)
                act.wait_ge(wdt_mm, 1)
                for i in range(G):
                    nc.scalar.activation(wdt_out[:, i, :], ps[:, i, :], ACT.Identity).then_inc(wdt_ev, 1)

            @block.tensor
            def _(pe):
                pe.wait_ge(ld, 16 * 9)
                pe.wait_ge(silu_done, 1)
                for m in range(MODS):
                    for k in range(G):
                        mm = nc.tensor.matmul(ps[0:NB, m, :], csilu[:, k, :], wmod_sb[:, k, m * D:(m + 1) * D],
                                              start=(k == 0), stop=(k == G - 1))
                mm.then_inc(mod_mm, 1)
                for g in range(G):
                    for k in range(G):
                        mm = nc.tensor.matmul(ps[:, 7, g:g + 1], wtau[:, k, g * P:(g + 1) * P], base[:, k:k + 1],
                                              start=(k == 0), stop=(k == G - 1))
                mm.then_inc(mod_mm, 1)
                pe.wait_ge(setup_v, 6)
                for i in range(G):
                    for k in range(G):
                        mm = nc.tensor.matmul(ps[:, i, :], wdT[:, k, i * P:(i + 1) * P], wtau[:, k, :],
                                              start=(k == 0), stop=(k == G - 1))
                mm.then_inc(wdt_mm, 1)

            @block.vector
            def _(dve):
                v = nc.vector
                count = [0]

                def done(ins):
                    count[0] += 1
                    ins.then_inc(setup_v, 1)

                dve.wait_ge(mod_mm, 1)
                for m, add in enumerate((0.0, 1.0, 0.0, 0.0, 1.0, 0.0)):
                    done(v.tensor_scalar(rows[0:NB, m, :], ps[0:NB, m, :], add, None, ALU.add))
                dve.wait_ge(setup_v, 6)
                for i, m in enumerate((2, 5)):
                    done(v.tensor_scalar(signs[0:NB, i, :], rows[0:NB, m, :], 0.0, 2.0, ALU.is_ge, ALU.mult))
                    done(v.scalar_tensor_tensor(mags[0:NB, i, :], rows[0:NB, m, :], -1.0, rows[0:NB, m, :], ALU.mult, ALU.max))
                dve.wait_ge(setup_v, 10)
                for i in range(2):
                    done(v.tensor_scalar(signs[0:NB, i, :], signs[0:NB, i, :], -1.0, None, ALU.add))
                    done(v.tensor_scalar(mags[0:NB, i, :], mags[0:NB, i, :], 0.25, None, ALU.max))
                dve.wait_ge(setup_v, 14)
                for i, m in enumerate((2, 5)):
                    done(v.tensor_tensor(rows[0:NB, m, :], signs[0:NB, i, :], mags[0:NB, i, :], ALU.mult))
                dve.wait_ge(mod_mm, 2)
                done(v.tensor_copy(tau_bias[:], ps[:, 7, 0:G]))
                dve.wait_ge(a_done, 1)
                done(v.tensor_scalar(negA[:], absA, -1.0, None, ALU.mult))
                done(v.tensor_scalar(halfA[:], absA, -0.5, None, ALU.mult))
                done(v.tensor_scalar(z_scale[:], absA, 1.0 / DA_EPS, None, ALU.mult))
                done(v.memset(consts[:, 0:1], -1.0))
                done(v.memset(consts[:, 1:2], LN_EPS))
                done(v.memset(consts[:, 2:3], 1e-18))
                dve.wait_ge(setup_v, count[0])
                done(v.reciprocal(recipA[:], negA[:]))
                dve.wait_ge(setup_v, count[0])

        c = Carve()
        xb = c(TT * D).rearrange("p (t d) -> p t d", t=TT)
        gate = xb.rearrange("p t d -> p (t d)").rearrange("p (g l) -> p g l", g=G)
        hT = c(G * L).rearrange("p (g l) -> p g l", g=G)
        valp = c(G * (L + 2)).rearrange("p (g l) -> p g l", g=G)
        win_sb = c(G * 2 * D).rearrange("p (k n) -> p k n", k=G)
        wdt_sb = c(G * D).rearrange("p (k n) -> p k n", k=G)
        wbc_sb = c(G * 2 * N).rearrange("p (k n) -> p k n", k=G)
        expo = hT
        lnw = valp[:, :, 0:L]

        c = Carve()
        zq = c(J * L).rearrange("p (j l) -> p j l", j=J)
        inv = c(J * L).rearrange("p (j l) -> p j l", j=J)
        th = c(J * L).rearrange("p (j l) -> p j l", j=J)
        abar = c(2 * J * L).rearrange("p (s j l) -> p s j l", s=2, j=J)
        bu = c(J * L).rearrange("p (j l) -> p j l", j=J)
        hs = c(J * L).rearrange("p (j l) -> p j l", j=J)
        gate_g = c(L)

        c = Carve()
        xc = c(TT * D).rearrange("p (t d) -> p t d", t=TT)
        wout_sb = c(G * D).rearrange("p (k n) -> p k n", k=G)
        mrows = c(3 * D).rearrange("p (m d) -> p m d", m=3)
        xn2 = c(2 * D).rearrange("p (s d) -> p s d", s=2)
        og2 = c(2 * D).rearrange("p (s d) -> p s d", s=2)

        x_in, w_in_s, st_bn, sqrt_done, xn_done, tr_done, hT_done = (
            [sem(f"x_loaded_{tb}") for tb in range(TB)], sem("weights_loaded"), sem("stats_done"), sem("sqrt_done"), sem("xn_done"),
            sem("transposed"), sem("hT_done"))
        z_mm, val_ev, gate_ev, conv_done, conv_v, u_done, gate_st = (
            sem("z_ready"), sem("val_evicted"), sem("gate_evicted"), sem("conv_done"), sem("conv_steps"), sem("u_done"),
            sem("gate_stored"))
        p_mm, p_ev, e_done, w_done, c_done, ln_done, sp_v, bc_mm, bc_v = (
            sem("p_ready"), sem("p_evicted"), sem("exp_done"), sem("one_plus_e_done"), sem("correction_done"),
            sem("ln_done"), sem("softplus_steps"), sem("bc_ready"), sem("bc_steps"))
        q_done, inv_sq, th_done, r3_done, bu_done, B_rdy, B_used, C_rdy, hC_done, y_done, sc_v, act_v, gl, yg_done = (
            sem("z_done"), sem("inv_ready"), sem("tanh_exp_ready"), sem("factor_done"), sem("bu_done"),
            sem("B_ready"), sem("B_used"), sem("C_ready"), sem("hC_done"), sem("y_summed"), sem("scan_steps"),
            sem("act_steps"), sem("gate_loaded"), sem("yg_done"))
        c_ld, o_mm, res_v, o_used, x1_done = (
            sem("resid_loads"), sem("out_ready"), sem("resid_steps"), sem("out_used"), sem("x1_done"))

        with nc.Fori(0, NB) as b:
            RING = 8
            z_groups = 2 * G * TB
            with nc.Block() as block:
                @block.sync
                def _(sp):
                    sp.wait_ge(x1_st, b * (16 * TB) + 16)
                    for tb in range(TB):
                        sp.dma_start(xb[:, tb * TPB:(tb + 1) * TPB, :],
                                     x[bass.ds(b, 1), tb * BANK:(tb + 1) * BANK, :].rearrange(
                                         "o (t p) d -> p (o t) d", p=P)).then_inc(x_in[tb], 16)
                    kp = "(k p) n -> p k n"
                    sp.dma_start(win_sb, W_in.rearrange(kp, p=P)).then_inc(w_in_s, 16)
                    sp.dma_start(wdt_sb, h_wdt.rearrange("p (k n) -> p k n", k=G)).then_inc(w_in_s, 16)
                    sp.dma_start(wbc_sb, W_BC.rearrange(kp, p=P)).then_inc(w_in_s, 16)
                    sp.dma_start(modT[:], h_mod[bass.ds(b, 1), :].rearrange("o (m g p) -> p (o m) g", m=MODS, p=P)).then_inc(w_in_s, 16)
                    for g in range(G):
                        sp.wait_ge(gate_ev, b * (G * TB) + (g + 1) * TB)
                        sp.dma_start(h_gate[g], gate[:, g, :]).then_inc(gate_st, 16)

                @block.scalar
                def _(act):
                    s = nc.scalar
                    act.wait_ge(st_bn, b * (2 * TT) + 2 * TT)
                    s.activation(spread[:], moments[:, :, 1], ACT.Sqrt, bias=consts[:, 1:2]).then_inc(sqrt_done, 1)
                    act.wait_ge(w_in_s, b * 64 + 64)
                    for tb in range(TB):
                        act.wait_ge(tr_done, b * TB + tb + 1)
                        for g in range(G):
                            s.activation(hT[:, g, tb * BANK:(tb + 1) * BANK], ps[:, (tb % 2) * G + g, :], ACT.Identity,
                                         bias=modT[:, 0, g:g + 1], scale=modT[:, 1, g:g + 1]).then_inc(hT_done, 1)
                    for g in range(G):
                        act.wait_ge(conv_done, b * G + g + 1)
                        s.activation(u[:, g, :], u[:, g, :], ACT.Silu).then_inc(u_done, 1)
                    for m in range(G):
                        for tb in range(TB):
                            r = (G + m) * TB + tb
                            act.wait_ge(z_mm, b * z_groups + r + 1)
                            s.activation(gate[:, m, tb * BANK:(tb + 1) * BANK], ps[:, r % RING, :],
                                         ACT.Silu).then_inc(gate_ev, 1)
                    for m in range(G):
                        for tb in range(TB):
                            r = z_groups + m * TB + tb
                            act.wait_ge(p_mm, b * (G * TB) + m * TB + tb + 1)
                            s.activation(delta[:, m, tb * BANK:(tb + 1) * BANK], ps[:, r % RING, :], ACT.Identity,
                                         bias=tau_bias[:, m:m + 1]).then_inc(p_ev, 1)
                    for m in range(G):
                        act.wait_ge(p_ev, b * (G * TB) + (m + 1) * TB)
                        s.activation(expo[:, m, :], delta[:, m, :], ACT.Abs).then_inc(act_v, 1)
                    for m in range(G):
                        act.wait_ge(act_v, b * G + m + 1)
                        s.activation(expo[:, m, :], expo[:, m, :], ACT.Exp, scale=-1.0).then_inc(e_done, 1)
                    for m in range(G):
                        act.wait_ge(c_done, b * G + m + 1)
                        s.activation(lnw[:, m, :], lnw[:, m, :], ACT.Ln).then_inc(ln_done, 1)

                @block.tensor
                def _(pe):
                    t = nc.tensor
                    for tb in range(TB):
                        pe.wait_ge(xn_done, b * TT + (tb + 1) * TPB)
                        if tb >= 2:
                            pe.wait_ge(hT_done, b * (G * TB) + (tb - 1) * G)
                        for tt in range(TPB):
                            for g in range(G):
                                mm = t.transpose(ps[:, (tb % 2) * G + g, tt * P:(tt + 1) * P],
                                                 xb[:, tb * TPB + tt, g * P:(g + 1) * P], identity[:])
                        mm.then_inc(tr_done, 1)
                    pe.wait_ge(w_in_s, b * 64 + 64)
                    pe.wait_ge(hT_done, b * (G * TB) + G * TB)
                    for m in range(2 * G):
                        for tb in range(TB):
                            r = m * TB + tb
                            if r >= RING:
                                old = r - RING
                                if old < G * TB:
                                    pe.wait_ge(val_ev, b * (G * TB) + old + 1)
                                else:
                                    pe.wait_ge(gate_ev, b * (G * TB) + old - G * TB + 1)
                            for k in range(G):
                                mm = t.matmul(ps[:, r % RING, :], win_sb[:, k, m * P:(m + 1) * P],
                                              hT[:, k, tb * BANK:(tb + 1) * BANK], start=(k == 0), stop=(k == G - 1))
                            mm.then_inc(z_mm, 1)
                    pe.wait_ge(u_done, b * G + G)
                    for m in range(G):
                        for tb in range(TB):
                            r = z_groups + m * TB + tb
                            old = r - RING
                            if old < z_groups:
                                pe.wait_ge(gate_ev, b * (G * TB) + old - G * TB + 1)
                            else:
                                pe.wait_ge(p_ev, b * (G * TB) + old - z_groups + 1)
                            for k in range(G):
                                mm = t.matmul(ps[:, r % RING, :], wdt_sb[:, k, m * P:(m + 1) * P],
                                              u[:, k, tb * BANK:(tb + 1) * BANK], start=(k == 0), stop=(k == G - 1))
                            mm.then_inc(p_mm, 1)
                    for tb in range(TB):
                        r = z_groups + G * TB + tb
                        pe.wait_ge(p_ev, b * (G * TB) + r - RING - z_groups + 1)
                        for k in range(G):
                            mm = t.matmul(ps[0:2 * N, r % RING, :], wbc_sb[:, k, :],
                                          u[:, k, tb * BANK:(tb + 1) * BANK], start=(k == 0), stop=(k == G - 1))
                        mm.then_inc(bc_mm, 1)

                @block.vector
                def _(dve):
                    v = nc.vector
                    for tb in range(TB):
                        dve.wait_ge(x_in[tb], b * 16 + 16)
                        for tt in range(tb * TPB, (tb + 1) * TPB):
                            v.bn_stats(stats[:, tt, :], xb[:, tt, :]).then_inc(st_bn, 1)
                    dve.wait_ge(st_bn, b * (2 * TT) + TT)
                    v.memset(valp[:, :, 0:1], 0.0)
                    v.memset(valp[:, :, L + 1:L + 2], 0.0).then_inc(sp_v, 1)
                    for tt in range(TT):
                        v.bn_aggr(moments[:, tt, :], stats[:, tt, :]).then_inc(st_bn, 1)
                    dve.wait_ge(sqrt_done, b + 1)
                    v.reciprocal(rstd[:], spread[:]).then_inc(sp_v, 1)
                    dve.wait_ge(sp_v, b * (2 + 2 * G) + 2)
                    for tt in range(TT):
                        v.tensor_scalar(xb[:, tt, :], xb[:, tt, :], moments[:, tt, 0:1], rstd[:, tt:tt + 1],
                                        ALU.subtract, ALU.mult).then_inc(xn_done, 1)
                    for g in range(G):
                        for tb in range(TB):
                            r = g * TB + tb
                            dve.wait_ge(z_mm, b * z_groups + r + 1)
                            v.tensor_copy(valp[:, g, 1 + tb * BANK:1 + (tb + 1) * BANK], ps[:, r % RING, :]).then_inc(val_ev, 1)
                        dve.wait_ge(val_ev, b * (G * TB) + (g + 1) * TB)
                        v.tensor_scalar(u[:, g, :], valp[:, g, 0:L], conv_taps[:, g, 0:1], None, ALU.mult).then_inc(conv_v, 1)
                        dve.wait_ge(conv_v, b * (2 * G) + 2 * g + 1)
                        v.scalar_tensor_tensor(u[:, g, :], valp[:, g, 1:L + 1], conv_taps[:, g, 1:2], u[:, g, :],
                                               ALU.mult, ALU.add).then_inc(conv_v, 1)
                        dve.wait_ge(conv_v, b * (2 * G) + 2 * g + 2)
                        v.scalar_tensor_tensor(u[:, g, :], valp[:, g, 2:L + 2], conv_taps[:, g, 2:3], u[:, g, :],
                                               ALU.mult, ALU.add).then_inc(conv_done, 1)
                    for tb in range(TB):
                        r = z_groups + G * TB + tb
                        cols = slice(tb * BANK, (tb + 1) * BANK)
                        n0 = 6 * tb

                        def own(k):
                            dve.wait_ge(bc_v, b * (6 * TB) + n0 + k)

                        dve.wait_ge(bc_mm, b * TB + tb + 1)
                        if tb:
                            own(0)
                        v.tensor_copy(BC3[0:2 * N, cols], ps[0:2 * N, r % RING, :]).then_inc(bc_v, 1)
                        own(1)
                        v.tensor_tensor(split[:, 0, :], ps[0:2 * N, r % RING, :], BC3[0:2 * N, cols], ALU.subtract).then_inc(bc_v, 1)
                        own(2)
                        v.tensor_copy(mid16[:], split[:, 0, :]).then_inc(bc_v, 1)
                        own(3)
                        v.tensor_tensor(split[:, 1, :], split[:, 0, :], mid16[:], ALU.subtract).then_inc(bc_v, 1)
                        own(4)
                        v.tensor_copy(BC3[2 * N:4 * N, cols], mid16[:]).then_inc(bc_v, 1)
                        v.tensor_copy(BC3[4 * N:6 * N, cols], split[:, 1, :]).then_inc(bc_v, 1)
                    for m in range(G):
                        dve.wait_ge(e_done, b * G + m + 1)
                        v.tensor_scalar(lnw[:, m, :], expo[:, m, :], 1.0, None, ALU.add).then_inc(w_done, 1)
                    for m in range(G):
                        dve.wait_ge(w_done, b * G + m + 1)
                        v.scalar_tensor_tensor(expo[:, m, :], lnw[:, m, :], -1.0, expo[:, m, :], ALU.add,
                                               ALU.subtract).then_inc(c_done, 1)
                    for m in range(G):
                        dve.wait_ge(ln_done, b * G + m + 1)
                        v.tensor_tensor(lnw[:, m, :], lnw[:, m, :], expo[:, m, :], ALU.subtract).then_inc(sp_v, 1)
                    for m in range(G):
                        dve.wait_ge(sp_v, b * (2 + 2 * G) + 2 + m + 1)
                        v.scalar_tensor_tensor(delta[:, m, :], delta[:, m, :], 0.0, lnw[:, m, :], ALU.max,
                                               ALU.add).then_inc(sp_v, 1)

            with nc.Fori(0, G) as g:
                it = b * G + g
                with nc.Block() as block:
                    @block.sync
                    def _(sp):
                        sp.wait_ge(gate_st, b * (16 * G) + 16 * G)
                        sp.dma_start(gate_g, h_gate[bass.ds(g, 1), :, :].rearrange("o p l -> p (o l)")).then_inc(gl, 16)

                    @block.scalar
                    def _(act):
                        s = nc.scalar
                        d_g = delta[:, bass.ds(g, 1), :].rearrange("p o l -> p (o l)")
                        for k in range(NK):
                            act.wait_ge(q_done, it * NK + k + 1)
                            if k:
                                act.wait_ge(r3_done, it * NK + k)
                            s.activation(inv, zq, ACT.Square, bias=consts[:, 0:1]).then_inc(inv_sq, 1)
                            act.wait_ge(inv_sq, it * (3 * NK) + 3 * k + 1)
                            s.activation(inv, inv, ACT.Ln, bias=consts[:, 2:3]).then_inc(inv_sq, 1)
                            act.wait_ge(inv_sq, it * (3 * NK) + 3 * k + 2)
                            s.activation(inv, inv, ACT.Exp, scale=-1.0).then_inc(inv_sq, 1)
                            if k:
                                act.wait_ge(bu_done, it * NK + k)
                            for j in range(J):
                                col = bass.ds(g * N + (k * J + j), 1)
                                s.activation(th[:, j, :], d_g, ACT.Tanh, scale=halfA[:, col])
                                s.activation(abar[:, k % 2, j, :], d_g, ACT.Exp, scale=negA[:, col]).then_inc(th_done, 1)

                    @block.tensor
                    def _(pe):
                        t = nc.tensor

                        def spread_row(row, bank, half, ready):
                            for h in range(2):
                                lo = half * HALF + h * BANK
                                mm = t.matmul(ps[:, bank + h, :], pick[:, row * P:(row + 1) * P], BC3[:, lo:lo + BANK],
                                              start=True, stop=True)
                            mm.then_inc(ready, 1)

                        spread_row(0, 0, 0, B_rdy)
                        for n in range(N):
                            k, j = divmod(n, J)
                            if j == 0:
                                for i in range(2 * J):
                                    w = 2 * J * k + i
                                    if w:
                                        pe.wait_ge(B_used, it * (2 * N) + w)
                                        spread_row(w // 2, 0, w % 2, B_rdy)
                            for half in range(2):
                                w = 2 * n + half
                                if w:
                                    pe.wait_ge(hC_done, it * (2 * N) + w)
                                spread_row(N + n, 2, half, C_rdy)
                                pe.wait_ge(hC_done, it * (2 * N) + w + 1)
                                for h in range(2):
                                    lo = half * HALF + h * BANK
                                    mm = t.matmul(ps[:, 4 + 2 * half + h, :], identity[:], hs[:, n % J, lo:lo + BANK],
                                                  start=(n == 0), stop=(n == N - 1), skip_group_check=True)
                                mm.then_inc(y_done, 1)

                    @block.vector
                    def _(dve):
                        v = nc.vector
                        d_g = delta[:, bass.ds(g, 1), :].rearrange("p o l -> p (o l)")
                        u_g = u[:, bass.ds(g, 1), :].rearrange("p o l -> p (o l)")
                        SV = 4 * NK + 1

                        def make_z(k):
                            for j in range(J):
                                mm = v.tensor_scalar(zq[:, j, :], d_g, z_scale[:, bass.ds(g * N + (k * J + j), 1)], Z_CAP,
                                                     ALU.mult, ALU.min)
                            mm.then_inc(q_done, 1)

                        dve.wait_ge(gate_st, b * (16 * G) + 16 * G)
                        make_z(0)
                        for k in range(NK):
                            dve.wait_ge(inv_sq, it * (3 * NK) + 3 * k + 3)
                            dve.wait_ge(q_done, it * NK + k + 1)
                            v.scalar_tensor_tensor(inv, zq, -1.0, inv, ALU.add, ALU.mult).then_inc(sc_v, 1)
                            dve.wait_ge(th_done, it * N + (k + 1) * J)
                            v.scalar_tensor_tensor(th, abar[:, k % 2], 1.0, th, ALU.add, ALU.mult).then_inc(sc_v, 1)
                            dve.wait_ge(sc_v, it * SV + 4 * k + 2)
                            v.scalar_tensor_tensor(th, inv, 1.0, th, ALU.add, ALU.mult).then_inc(r3_done, 1)
                            if k < NK - 1:
                                make_z(k + 1)
                            for j in range(J):
                                for half in range(2):
                                    w = (k * J + j) * 2 + half
                                    dve.wait_ge(B_rdy, it * (2 * N) + w + 1)
                                    cols = slice(half * HALF, (half + 1) * HALF)
                                    v.scalar_tensor_tensor(
                                        bu[:, j, cols], u[:, bass.ds(g, 1), cols].rearrange("p o l -> p (o l)"),
                                        recipA[:, bass.ds(g * N + (k * J + j), 1)],
                                        ps[:, 0:2, :].rearrange("p a l -> p (a l)"), ALU.mult, ALU.mult).then_inc(B_used, 1)
                            dve.wait_ge(B_used, it * (2 * N) + (k + 1) * 2 * J)
                            dve.wait_ge(r3_done, it * NK + k + 1)
                            v.tensor_tensor(bu, bu, th, ALU.mult).then_inc(bu_done, 1)
                            dve.wait_ge(bu_done, it * NK + k + 1)
                            for j in range(J):
                                n = k * J + j
                                if n >= J:
                                    dve.wait_ge(y_done, it * (2 * N) + 2 * (n - J) + 2)
                                v.tensor_tensor_scan(hs[:, j, :], abar[:, k % 2, j, :], bu[:, j, :], 0.0, ALU.mult,
                                                     ALU.add).then_inc(sc_v, 1)
                                dve.wait_ge(sc_v, it * SV + 4 * k + 3 + j)
                                for half in range(2):
                                    w = 2 * n + half
                                    cols = slice(half * HALF, (half + 1) * HALF)
                                    dve.wait_ge(C_rdy, it * (2 * N) + w + 1)
                                    v.tensor_tensor(hs[:, j, cols], hs[:, j, cols],
                                                    ps[:, 2:4, :].rearrange("p a l -> p (a l)"), ALU.mult).then_inc(hC_done, 1)
                        dve.wait_ge(y_done, it * (2 * N) + 2 * N)
                        dve.wait_ge(gl, it * 16 + 16)
                        v.tensor_tensor(u_g, ps[:, 4:8, :].rearrange("p a l -> p (a l)"), gate_g, ALU.mult).then_inc(sc_v, 1)

            with nc.Block() as block:
                @block.sync
                def _(sp):
                    for m in range(3):
                        sp.dma_start(mrows[:, m, :], h_mod[bass.ds(b, 1), m * D:(m + 1) * D].partition_broadcast(P)
                                     .rearrange("p o d -> p (o d)")).then_inc(c_ld, 16)
                    sp.dma_start(wout_sb, W_out.rearrange("(k p) n -> p k n", p=P)).then_inc(c_ld, 16)
                    for tb in range(TB):
                        sp.dma_start(xc[:, tb * TPB:(tb + 1) * TPB, :],
                                     x[bass.ds(b, 1), tb * BANK:(tb + 1) * BANK, :].rearrange(
                                         "o (t p) d -> p (o t) d", p=P)).then_inc(c_ld, 16)
                    for tb in range(TB):
                        sp.wait_ge(x1_done, b * TT + (tb + 1) * TPB)
                        sp.dma_start(h_x1[bass.ds(b * L + tb * BANK, BANK), :].rearrange("(t p) d -> p t d", p=P),
                                     xc[:, tb * TPB:(tb + 1) * TPB, :]).then_inc(x1_st, 16)

                @block.tensor
                def _(pe):
                    pe.wait_ge(c_ld, b * (16 * (4 + TB)) + 16 * (4 + TB))
                    for tt in range(TT):
                        if tt >= RING:
                            pe.wait_ge(o_used, b * TT + tt - RING + 1)
                        for k in range(G):
                            mm = nc.tensor.matmul(ps[:, tt % RING, :], u[:, k, tt * P:(tt + 1) * P], wout_sb[:, k, :],
                                                  start=(k == 0), stop=(k == G - 1))
                        mm.then_inc(o_mm, 1)

                @block.vector
                def _(dve):
                    v = nc.vector
                    SV = 2 + 4 * TT
                    sa, ca1, ga = mrows[:, 0, :], mrows[:, 1, :], mrows[:, 2, :]
                    dve.wait_ge(c_ld, b * (16 * (4 + TB)) + 16 * (4 + TB))
                    v.tensor_tensor(sa, sa, ga, ALU.mult).then_inc(res_v, 1)
                    v.tensor_tensor(ca1, ca1, ga, ALU.mult).then_inc(res_v, 1)
                    dve.wait_ge(res_v, b * SV + 2)
                    for tt in range(TT):
                        n0 = 2 + 4 * tt
                        xn, og = xn2[:, tt % 2, :], og2[:, tt % 2, :]
                        v.tensor_scalar(xn, xc[:, tt, :], moments[:, tt, 0:1], rstd[:, tt:tt + 1], ALU.subtract,
                                        ALU.mult).then_inc(res_v, 1)
                        v.tensor_tensor(xc[:, tt, :], xc[:, tt, :], sa, ALU.add).then_inc(res_v, 1)
                        dve.wait_ge(o_mm, b * TT + tt + 1)
                        v.tensor_tensor(og, ps[:, tt % RING, :], ga, ALU.mult).then_inc(o_used, 1)
                        dve.wait_ge(res_v, b * SV + n0 + 2)
                        v.tensor_tensor(xn, xn, ca1, ALU.mult).then_inc(res_v, 1)
                        dve.wait_ge(o_used, b * TT + tt + 1)
                        v.tensor_tensor(xc[:, tt, :], xc[:, tt, :], og, ALU.add).then_inc(res_v, 1)
                        dve.wait_ge(res_v, b * SV + n0 + 4)
                        v.tensor_tensor(xc[:, tt, :], xc[:, tt, :], xn, ALU.add).then_inc(x1_done, 1)

        c = Carve()
        w1_sb = c(G * EX * HID).rearrange("p (k n) -> p k n", k=G)
        w2_sb = c(EX * HT * D).rearrange("p (e n) -> p e n", e=EX * HT)
        x1 = c(TPB * D).rearrange("p (t d) -> p t d", t=TPB)
        xn = c(TPB * D).rearrange("p (t d) -> p t d", t=TPB)
        h2T = c(G * BANK).rearrange("p (g l) -> p g l", g=G)
        hid = c(2 * HT * BANK).rearrange("p (s h l) -> p s h l", s=2, h=HT)
        acc = xn
        gbrow = c(D)
        gw_sb = c(G * E).rearrange("p (k e) -> p k e", k=G)
        b1_sb = c(EX * HT)
        b2_sb = c(D)
        rs_sb = c(1)
        sco = c(TPB * E).rearrange("p (t e) -> p t e", t=TPB)
        low = c(E * E).rearrange("p (e f) -> p e f", e=E)
        above = c(TPB * E * E).rearrange("p (t e f) -> p t e f", t=TPB, e=E)
        ties = c(TPB * E * E).rearrange("p (t e f) -> p t e f", t=TPB, e=E)
        rank = c(TPB * E).rearrange("p (t e) -> p t e", t=TPB)
        gates = c(TPB * EX).rearrange("p (t e) -> p t e", t=TPB)
        gsum = c(TPB)
        grec = c(TPB)
        gT = c(BANK)

        f_ld, f_x, f_v, f_sqrt, f_tr, f_h2, f_gm, f_sig, f_gates, f_gT, f_gTv, f_w1, f_gelu, f_w2, f_acc, f_st = (
            sem("ffn_weights"), sem("ffn_x1"), sem("ffn_steps"), sem("ffn_sqrt"), sem("ffn_transposed"), sem("h2_done"),
            sem("gate_logits"), sem("scores_done"), sem("gates_done"), sem("gates_transposed"), sem("gates_copied"),
            sem("w1_ready"), sem("hidden_done"), sem("w2_ready"), sem("acc_done"), sem("xn_free_or_stored"))

        with nc.Block() as block:
            @block.sync
            def _(sp):
                kp = "(k p) n -> p k n"
                sp.wait_ge(x1_st, NB * 16 * TB + 16)
                sp.dma_start(w1_sb, W1.rearrange(kp, p=P)).then_inc(f_ld, 16)
                sp.dma_start(w2_sb, W2.rearrange(kp, p=P)).then_inc(f_ld, 16)
                sp.dma_start(gw_sb, gate_W.rearrange(kp, p=P)).then_inc(f_ld, 16)
                sp.dma_start(b1_sb, b1.rearrange("(k p) -> p k", p=P)).then_inc(f_ld, 16)
                sp.dma_start(b2_sb[0:EX, :], b2).then_inc(f_ld, 16)
                sp.dma_start(rs_sb, route_scale.partition_broadcast(P)).then_inc(f_ld, 16)
                sp.dma_start(low.rearrange("p e f -> p (e f)"), earlier.partition_broadcast(P)).then_inc(f_ld, 16)
                sp.wait_ge(f_ld, 16 * 7)

            @block.vector
            def _(dve):
                nc.vector.memset(gates[:, :, E:EX], 1.0).then_inc(f_st, 1)

        FV = 3 * TPB + 9
        AV = 1 + (EX + 3) * TPB
        out_flat = out.rearrange("b l d -> (b l) d")
        with nc.Fori(0, NB) as fb:
            with nc.Fori(0, TB) as tb:
                i = fb * TB + tb
                with nc.Block() as block:
                    @block.sync
                    def _(sp):
                        sp.dma_start(x1, h_x1[bass.ds(i * BANK, BANK), :].rearrange("(t p) d -> p t d", p=P)).then_inc(f_x, 16)
                        sp.dma_start(modT[:], h_mod[bass.ds(fb, 1), :].rearrange("o (m g p) -> p (o m) g", m=MODS, p=P)).then_inc(f_x, 16)
                        sp.dma_start(gbrow, h_mod[bass.ds(fb, 1), 5 * D:6 * D].partition_broadcast(P)
                                     .rearrange("p o d -> p (o d)")).then_inc(f_x, 16)
                        sp.wait_ge(f_acc, i * AV + AV)
                        sp.dma_start(out_flat[bass.ds(i * BANK, BANK), :].rearrange("(t p) d -> p t d", p=P), xn).then_inc(f_st, 16)

                    @block.scalar
                    def _(act):
                        s = nc.scalar
                        act.wait_ge(f_v, i * FV + 2 * TPB)
                        s.activation(spread[:, 0:TPB], moments[:, 0:TPB, 1], ACT.Sqrt, bias=consts[:, 1:2]).then_inc(f_sqrt, 1)
                        act.wait_ge(f_tr, i + 1)
                        for g in range(G):
                            s.activation(h2T[:, g, :], ps[:, g, :], ACT.Identity, bias=modT[:, 3, g:g + 1],
                                         scale=modT[:, 4, g:g + 1]).then_inc(f_h2, 1)
                        act.wait_ge(f_gm, i + 1)
                        s.activation(sco.rearrange("p t e -> p (t e)"), ps[:, 4, 0:TPB * E], ACT.Sigmoid).then_inc(f_sig, 1)
                        for e in range(EX):
                            if e >= 2:
                                act.wait_ge(f_w2, i * (EX * TPB + TPB) + (e - 1) * TPB)
                            for h in range(HT):
                                act.wait_ge(f_w1, i * (EX * HT) + e * HT + h + 1)
                                s.activation(hid[:, e % 2, h, :], ps[:, h, :], ACT.Gelu,
                                             bias=b1_sb[:, e * HT + h:e * HT + h + 1]).then_inc(f_gelu, 1)

                    @block.tensor
                    def _(pe):
                        t = nc.tensor
                        pe.wait_ge(f_v, i * FV + 3 * TPB + 1)
                        for tt in range(TPB):
                            for g in range(G):
                                mm = t.transpose(ps[:, g, tt * P:(tt + 1) * P], xn[:, tt, g * P:(g + 1) * P], identity[:])
                        mm.then_inc(f_tr, 1)
                        pe.wait_ge(f_h2, i * G + G)
                        for tt in range(TPB):
                            for k in range(G):
                                mm = t.matmul(ps[:, 4, tt * E:(tt + 1) * E], h2T[:, k, tt * P:(tt + 1) * P], gw_sb[:, k, :],
                                              start=(k == 0), stop=(k == G - 1))
                        mm.then_inc(f_gm, 1)

                        def up(e):
                            for h in range(HT):
                                if e:
                                    pe.wait_ge(f_gelu, i * (EX * HT) + (e - 1) * HT + h + 1)
                                for k in range(G):
                                    col = (e * HT + h) * P
                                    mm = t.matmul(ps[:, h, :], w1_sb[:, k, col:col + P], h2T[:, k, :], start=(k == 0),
                                                  stop=(k == G - 1))
                                mm.then_inc(f_w1, 1)

                        up(0)
                        pe.wait_ge(f_gates, i + 1)
                        for tt in range(TPB):
                            mm = t.transpose(ps[0:EX, 5, tt * P:(tt + 1) * P], gates[:, tt, :], identity[:])
                        mm.then_inc(f_gT, 1)
                        pe.wait_ge(f_gTv, i + 1)
                        for tt in range(TPB):
                            t.matmul(ps[:, 4 + tt, :], gT[0:EX, tt * P:(tt + 1) * P], b2_sb[0:EX, :], start=True,
                                     stop=True).then_inc(f_w2, 1)
                        for e in range(EX):
                            if e + 1 < EX:
                                up(e + 1)
                            pe.wait_ge(f_gelu, i * (EX * HT) + (e + 1) * HT)
                            for tt in range(TPB):
                                pe.wait_ge(f_acc, i * AV + 1 + e * TPB + tt + 1)
                                for h in range(HT):
                                    mm = t.matmul(ps[:, 4 + tt, :], hid[:, e % 2, h, tt * P:(tt + 1) * P],
                                                  w2_sb[:, e * HT + h, :], start=(h == 0), stop=(h == HT - 1))
                                mm.then_inc(f_w2, 1)

                    @block.vector
                    def _(dve):
                        v = nc.vector
                        n = [0]

                        def step(ins):
                            n[0] += 1
                            ins.then_inc(f_v, 1)

                        def own():
                            dve.wait_ge(f_v, i * FV + n[0])

                        dve.wait_ge(f_x, i * 48 + 48)
                        for tt in range(TPB):
                            step(v.bn_stats(stats[:, tt, :], x1[:, tt, :]))
                        own()
                        v.memset(gates[:, :, E:EX], 1.0)
                        for tt in range(TPB):
                            step(v.bn_aggr(moments[:, tt, :], stats[:, tt, :]))
                        dve.wait_ge(f_sqrt, i + 1)
                        step(v.reciprocal(rstd[:, 0:TPB], spread[:, 0:TPB]))
                        own()
                        dve.wait_ge(f_st, i * 16 + 1)
                        for tt in range(TPB):
                            step(v.tensor_scalar(xn[:, tt, :], x1[:, tt, :], moments[:, tt, 0:1], rstd[:, tt:tt + 1],
                                                 ALU.subtract, ALU.mult))
                        dve.wait_ge(f_sig, i + 1)
                        step(v.tensor_scalar(sco, sco, rs_sb[:, 0:1], None, ALU.mult))
                        own()
                        other = sco.unsqueeze(2).broadcast_to([P, TPB, E, E])
                        mine = sco.unsqueeze(3).broadcast_to([P, TPB, E, E])
                        step(v.tensor_tensor(above, other, mine, ALU.is_gt))
                        step(v.tensor_tensor(ties, other, mine, ALU.is_equal))
                        own()
                        step(v.tensor_tensor(ties, ties, low.unsqueeze(1).broadcast_to([P, TPB, E, E]), ALU.mult))
                        own()
                        step(v.tensor_tensor(above, above, ties, ALU.add))
                        own()
                        step(v.tensor_reduce(rank, above, AX_X, ALU.add))
                        own()
                        step(v.scalar_tensor_tensor(gates[:, :, 0:E], rank, 1.5, sco, ALU.is_lt, ALU.mult))
                        own()
                        step(v.tensor_reduce(gsum, gates[:, :, 0:E], AX_X, ALU.add))
                        assert n[0] == FV, (n[0], FV)
                        own()
                        v.reciprocal(grec, gsum).then_inc(f_acc, 1)
                        dve.wait_ge(f_acc, i * AV + 1)
                        v.tensor_tensor(gates[:, :, 0:E], gates[:, :, 0:E], grec.unsqueeze(2).broadcast_to([P, TPB, E]),
                                        ALU.mult).then_inc(f_gates, 1)
                        dve.wait_ge(f_gT, i + 1)
                        v.tensor_copy(gT[0:EX, :], ps[0:EX, 5, :]).then_inc(f_gTv, 1)
                        dve.wait_ge(f_gates, i + 1)
                        for tt in range(TPB):
                            dve.wait_ge(f_w2, i * (EX * TPB + TPB) + tt + 1)
                            v.tensor_copy(acc[:, tt, :], ps[:, 4 + tt, :]).then_inc(f_acc, 1)
                        for e in range(EX):
                            for tt in range(TPB):
                                w = (e + 1) * TPB + tt
                                dve.wait_ge(f_w2, i * (EX * TPB + TPB) + w + 1)
                                dve.wait_ge(f_acc, i * AV + 1 + e * TPB + tt + 1)
                                v.scalar_tensor_tensor(acc[:, tt, :], ps[:, 4 + tt, :], gates[:, tt, e:e + 1],
                                                       acc[:, tt, :], ALU.mult, ALU.add).then_inc(f_acc, 1)
                        for tt in range(TPB):
                            dve.wait_ge(f_acc, i * AV + 1 + EX * TPB + tt + 1)
                            v.tensor_tensor(acc[:, tt, :], acc[:, tt, :], gbrow, ALU.mult).then_inc(f_acc, 1)
                        for tt in range(TPB):
                            dve.wait_ge(f_acc, i * AV + 1 + (EX + 1) * TPB + tt + 1)
                            v.tensor_tensor(acc[:, tt, :], acc[:, tt, :], x1[:, tt, :], ALU.add).then_inc(f_acc, 1)

        with nc.Block() as block:
            @block.sync
            def _(sp):
                sp.wait_ge(f_st, 16 * NBLK + 1)


def kernel(**inputs):
    import numpy as _np
    import concourse.bacc as _bacc
    from concourse import mybir as _mybir
    from concourse.bass_utils import run_bass_kernel_spmd as _run

    a = {k: _np.asarray(v) for k, v in inputs.items()}
    D = a["L0_attn_x"].shape[2]
    N = a["L0_attn_A_log"].shape[1]
    E, _, H = a["L0_ffn_W1"].shape
    c = _np.ascontiguousarray
    laid = {
        "x": a["L0_attn_x"],
        "W_in": a["L0_attn_W_in"],
        "conv_w": a["L0_attn_conv_w"][:, 0, :],
        "W_BC": _np.concatenate([a["L0_attn_W_B"], a["L0_attn_W_C"]], axis=1),
        "W_deltaT": a["L0_attn_W_delta"].T,
        "delta_base": a["L0_attn_delta_base"],
        "W_tau": a["L0_attn_W_tau"],
        "A_log": a["L0_attn_A_log"],
        "W_out": a["L0_attn_W_out"],
        "gate_W": a["L0_ffn_gate_W"],
        "W1": _np.concatenate([a["L0_ffn_W1"].transpose(1, 0, 2).reshape(D, E * H), a["L0_ffn_Ws1"]], axis=1),
        "b1": _np.concatenate([a["L0_ffn_b1"].reshape(E * H), a["L0_ffn_bs1"]]),
        "W2": _np.concatenate([a["L0_ffn_W2"].reshape(E * H, D), a["L0_ffn_Ws2"]], axis=0),
        "b2": _np.concatenate([a["L0_ffn_b2"], a["L0_ffn_bs2"][None, :]], axis=0),
        "route_scale": a["L0_ffn_route_scale"].reshape(1),
        "cT": a["L0_c"].T,
        "wmod": a["L0_wmod"],
        "ident": _np.eye(128, dtype=_np.float32),
        "onehot": _np.repeat(_np.tile(_np.eye(2 * N, dtype=_np.float32), (3, 1)), 128, axis=1).astype(_mybir.dt.np(_mybir.dt.bfloat16)),
        "earlier": _np.tril(_np.ones((E, E), _np.float32), -1).reshape(E * E),
    }
    nc = _bacc.Bacc("TRN2", target_bir_lowering=False, num_devices=1)
    arrays, args = {}, []
    for name, arr in laid.items():
        arr = c(arr)
        arrays[f"in_{name}"] = arr
        args.append(nc.dram_tensor(f"in_{name}", arr.shape, _mybir.dt.from_np(arr.dtype), kind="ExternalInput").ap())
    args.append(nc.dram_tensor("out_0", a["L0_attn_x"].shape, _mybir.dt.float32, kind="ExternalOutput").ap())
    adaln_mamba_moe(nc, *args)
    r = _run(nc, [arrays], core_ids=[0])
    return r.results[0]["out_0"]
```

```python
from contextlib import ExitStack

import numpy as np
import concourse.bass as bass
from concourse import mybir

ALU = mybir.AluOpType
ACT = mybir.ActivationFunctionType
F32 = mybir.dt.float32
BF16 = mybir.dt.bfloat16
AX_X = mybir.AxisListType.X

P = 128
BANK = 512
LN_EPS = 1e-5
DA_EPS = float(np.float32(1e-6))
Z_CAP = 4e9


def adaln_mamba_moe(nc, x, W_in, conv_w, W_BC, W_deltaT, delta_base, W_tau, A_log, W_out, gate_W, W1, b1, W2, b2,
                    route_scale, cT, wmod, ident, onehot, earlier, keep, out):
    NB, L, D = x.shape
    G = D // P
    N = A_log.shape[1]
    T = BANK
    TPB = T // P
    NBLK = NB * L // T
    PER = L // T
    E = gate_W.shape[1]
    EX = E + 1
    HID = W1.shape[1] // EX
    HT = HID // P
    MODS = wmod.shape[1] // D
    ROWS = MODS + 2
    R_SAGA, R_CAGA, R_GA, R_GB = 6, 7, 2, 5

    h_rows = nc.dram_tensor("row_scratch", [NBLK, ROWS * D], F32).ap()
    h_wdt = nc.dram_tensor("w_delta_tau_scratch", [P, G * D], F32).ap()
    x_flat = x.rearrange("b l d -> (b l) d")
    out_flat = out.rearrange("b l d -> (b l) d")

    with ExitStack() as ctx:
        ctx.enter_context(nc.allow_non_contiguous_dma(reason="small per-channel tables"))

        def sb(name, shape, dt=F32):
            return ctx.enter_context(nc.sbuf_tensor(name, shape, dt))

        def sem(name):
            return ctx.enter_context(nc.semaphore(name))

        def ge(eng, s, value):
            if not isinstance(value, int) or value > 0:
                eng.wait_ge(s, value)

        ps = ctx.enter_context(nc.psum_tensor("ps", [P, 8, BANK], F32))
        Y_BANK, B_BANK, C_BANK, JOB_BANK = 0, 4, 5, 6

        identity = sb("identity", [P, P])
        pick = sb("pick", [3 * 2 * N, 2 * N], BF16)
        conv_taps = sb("conv_taps", [P, G, 3])
        negA = sb("negA", [P, N, G])
        halfA = sb("halfA", [P, N, G])
        z_scale = sb("z_scale", [P, N, G])
        recipA = sb("recipA", [P, N, G])
        tau_bias = sb("tau_bias", [P, G])
        consts = sb("consts", [P, 3])
        halo = sb("halo", [P, G, 2 * NBLK])
        keep_lim = sb("keep_lim", [P, 2, NBLK])
        low = sb("low", [P, E, E])
        b1_sb = sb("b1_sb", [P, EX * HT])
        b2_sb = sb("b2_sb", [EX, D])
        gw_sb = sb("gw_sb", [P, G, E])
        rs_sb = sb("rs_sb", [P, 1])
        win_sb = sb("win_sb", [P, G, 2 * D])
        wdt_sb = sb("wdt_sb", [P, G, D])
        wbc_sb = sb("wbc_sb", [P, G, 2 * N])
        wout_sb = sb("wout_sb", [P, G, D])
        w1_e = sb("w1_e", [P, 2, G, HID])
        w2_e = sb("w2_e", [P, 2, HT, D])
        zq = sb("zq", [P, G, T])
        inv = sb("inv", [P, 2, G, T])
        th = sb("th", [P, 2, G, T])
        abar = sb("abar", [P, 2, G, T])
        hs = sb("hs", [P, G, T])
        carry = sb("carry", [P, N, G])
        u = sb("u", [P, G, T])
        delta = sb("delta", [P, G, T])
        BC3 = sb("BC3", [3 * 2 * N, T], BF16)
        u_next = sb("u_next", [P, G, T])
        delta_next = sb("delta_next", [P, G, T])
        BC3_next = sb("BC3_next", [3 * 2 * N, T], BF16)
        valp = sb("valp", [P, G, T + 2])
        modA = sb("modA", [P, 5, G])
        stats = sb("stats", [P, TPB, 6])
        momA = sb("momA", [P, TPB, 2])
        spreadA = sb("spreadA", [P, TPB])
        norms = sb("norms", [P, NBLK, TPB, 2])
        ys = sb("ys", [P, G, T])
        x1 = sb("x1", [P, TPB, D])
        xn = sb("xn", [P, TPB, D])
        hf = sb("hf", [P, G, T])
        hid = sb("hid", [P, 2, HT, T])
        rows = sb("rows", [P, 3, D])
        modF = sb("modF", [P, 5, G])
        statsF = sb("statsF", [P, TPB, 6])
        momF = sb("momF", [P, TPB, 2])
        spreadF = sb("spreadF", [P, TPB])
        rstdF = sb("rstdF", [P, TPB])
        sco = sb("sco", [P, TPB, E])
        rank = sb("rank", [P, TPB, E])
        gates = sb("gates", [P, TPB, EX])
        gsum = sb("gsum", [P, TPB])

        def flat(ap):
            return ap.rearrange("p a b -> p (a b)")

        xa = flat(u_next[:]).rearrange("p (t d) -> p t d", t=TPB)
        hT = delta_next
        e_neg = ys
        lnw = flat(valp[:])[:, 0:G * T].rearrange("p (g t) -> p g t", g=G)
        gate = hid[:].rearrange("p s h t -> p (s h) t")
        gT = rows[:, 0, :]
        og = flat(hf[:]).rearrange("p (t d) -> p t d", t=TPB)
        zflat = flat(zq[:])
        split = zflat[0:2 * N, 0:2 * T].rearrange("p (s t) -> p s t", s=2)
        mid16 = zflat[0:2 * N, 2 * T:2 * T + T // 2].bitcast(BF16)
        above = zflat[:, 0:TPB * E * E].rearrange("p (t e f) -> p t e f", t=TPB, e=E)
        ties = zflat[:, TPB * E * E:2 * TPB * E * E].rearrange("p (t e f) -> p t e f", t=TPB, e=E)

        wmod_h = [inv[:].rearrange("p s g t -> p (s g t)"), th[:].rearrange("p s g t -> p (s g t)"),
                  abar[:].rearrange("p s g t -> p (s g t)")]
        wdT = flat(u[:]).rearrange("p (k n) -> p k n", k=G)
        wtau = flat(delta[:]).rearrange("p (k n) -> p k n", k=G)
        small = flat(zq[:])
        cs = small[:, 0:16].rearrange("p (k b) -> p k b", k=G)
        csilu = small[:, 16:32].rearrange("p (k b) -> p k b", k=G)
        base = small[:, 32:36]
        absA = small[:, 64:64 + N * G].rearrange("p (n g) -> p n g", n=N)
        alog = small[:, 128:128 + N * G].rearrange("p (g n) -> p g n", n=N)
        modh = small[:, 256:256 + 2 * G * NB].rearrange("p (m g b) -> p m g b", m=2, g=G)
        hh = small[:, 512:512 + G * 2 * NBLK].rearrange("p (g i) -> p g i", g=G)
        mrow = flat(x1[:])
        mrow2 = flat(xn[:])
        modrow = [mrow[:, m * D:(m + 1) * D] for m in range(4)] + [mrow2[:, m * D:(m + 1) * D] for m in range(4)]
        signs = flat(hf[:])[:, 0:2 * D].rearrange("p (m d) -> p m d", m=2)
        mags = flat(hf[:])[:, 2 * D:4 * D].rearrange("p (m d) -> p m d", m=2)
        hx = flat(hs[:])[:, 0:D]
        NH = 2 * NBLK

        ld, ld_pads, ld_mod = sem("setup_loads"), sem("halo_tokens_loaded"), sem("halo_rows_loaded")
        silu_done, a_done, mod_mm, wdt_mm, setup_v, rows_v, wdt_ev, st_rows, st_wdt, ld_wdt = (
            sem("silu_done"), sem("a_done"), sem("mod_mm"), sem("wdt_mm"), sem("setup_vector"), sem("rows_done"),
            sem("wdt_evicted"), sem("rows_stored"), sem("wdt_stored"), sem("wdt_loaded"))
        halo_v, halo_sq, halo_mm = sem("halo_steps"), sem("halo_sqrt"), sem("halo_products")
        LOADS = 20
        with nc.Block() as block:
            @block.sync
            def _(sp):
                kp = "(k p) n -> p k n"
                for r in range(3):
                    sp.dma_start(wmod_h[r].rearrange("p (k n) -> p k n", k=G),
                                 wmod[:, 2 * r * D:2 * (r + 1) * D].rearrange(kp, p=P)).then_inc(ld, 16)
                sp.dma_start(cs, cT.rearrange(kp, p=P)).then_inc(ld, 16)
                sp.dma_start(wdT, W_deltaT.rearrange(kp, p=P)).then_inc(ld, 16)
                sp.dma_start(wtau, W_tau.rearrange(kp, p=P)).then_inc(ld, 16)
                sp.dma_start(base, delta_base.rearrange("(k p) -> p k", p=P)).then_inc(ld, 16)
                sp.dma_start(alog, A_log.rearrange("(g p) n -> p g n", p=P)).then_inc(ld, 16)
                sp.dma_start(conv_taps[:], conv_w.rearrange("(g p) n -> p g n", p=P)).then_inc(ld, 16)
                sp.dma_start(identity[:], ident).then_inc(ld, 16)
                sp.dma_start(pick[:], onehot).then_inc(ld, 16)
                sp.dma_start(flat(keep_lim[:]), keep.partition_broadcast(P)).then_inc(ld, 16)
                sp.dma_start(flat(low[:]), earlier.partition_broadcast(P)).then_inc(ld, 16)
                sp.dma_start(b1_sb[:], b1.rearrange("(k p) -> p k", p=P)).then_inc(ld, 16)
                sp.dma_start(b2_sb[:], b2).then_inc(ld, 16)
                sp.dma_start(gw_sb[:], gate_W.rearrange(kp, p=P)).then_inc(ld, 16)
                sp.dma_start(rs_sb[:], route_scale.partition_broadcast(P)).then_inc(ld, 16)
                sp.dma_start(win_sb[:], W_in.rearrange(kp, p=P)).then_inc(ld, 16)
                sp.dma_start(wbc_sb[:], W_BC.rearrange(kp, p=P)).then_inc(ld, 16)
                sp.dma_start(wout_sb[:], W_out.rearrange(kp, p=P)).then_inc(ld, 16)
                xt = x_flat.rearrange("(i t) d -> i t d", t=T)
                sp.dma_start(hx[0:1, :], x_flat[0:1, :]).then_inc(ld_pads, 16)
                sp.dma_start(hx[1:NBLK, :], xt[0:NBLK - 1, T - 1, :]).then_inc(ld_pads, 16)
                sp.dma_start(hx[NBLK:NH - 1, :], xt[1:NBLK, 0, :]).then_inc(ld_pads, 16)
                sp.dma_start(hx[NH - 1:NH, :], x_flat[0:1, :]).then_inc(ld_pads, 16)
                sp.wait_ge(rows_v, 3)
                hr = h_rows.rearrange("(b r) (m d) -> r b m d", r=PER, m=ROWS)
                for r in range(PER):
                    sp.dma_start(hr[r, :, 0:4, :], mrow[0:NB, :].rearrange("b (m d) -> b m d", m=4)).then_inc(st_rows, 16)
                    sp.dma_start(hr[r, :, 4:8, :], mrow2[0:NB, :].rearrange("b (m d) -> b m d", m=4)).then_inc(st_rows, 16)
                sp.wait_ge(st_rows, 32 * PER)
                hb = h_rows.rearrange("(b r) (m g p) -> r m g p b", r=PER, m=ROWS, p=P)
                for m in range(2):
                    for g in range(G):
                        sp.dma_start(modh[:, m, g, :], hb[0, m, g]).then_inc(ld_mod, 16)
                sp.wait_ge(ld_mod, 32 * G)

            @block.scalar
            def _(act):
                act.wait_ge(ld, 16 * LOADS)
                nc.scalar.activation(csilu, cs, ACT.Silu).then_inc(silu_done, 1)
                for g in range(G):
                    ins = nc.scalar.activation(absA[:, :, g], alog[:, g, :], ACT.Exp)
                ins.then_inc(a_done, 1)
                act.wait_ge(halo_v, 2)
                nc.scalar.activation(spreadA[0:NH, 0:1], momA[0:NH, 0, 1:2], ACT.Sqrt, bias=consts[0:NH, 1:2]).then_inc(halo_sq, 1)
                act.wait_ge(wdt_mm, 1)
                for i in range(G):
                    nc.scalar.activation(wdt_sb[:, i, :], ps[:, i, :], ACT.Identity).then_inc(wdt_ev, 1)

            @block.tensor
            def _(pe):
                pe.wait_ge(ld, 16 * LOADS)
                pe.wait_ge(silu_done, 1)
                for m in range(MODS):
                    w = wmod_h[m // 2].rearrange("p (k n) -> p k n", k=G)
                    for k in range(G):
                        mm = nc.tensor.matmul(ps[0:NB, m, :], csilu[:, k, :], w[:, k, (m % 2) * D:(m % 2 + 1) * D],
                                              start=(k == 0), stop=(k == G - 1))
                mm.then_inc(mod_mm, 1)
                for g in range(G):
                    for k in range(G):
                        mm = nc.tensor.matmul(ps[:, 7, g:g + 1], wtau[:, k, g * P:(g + 1) * P], base[:, k:k + 1],
                                              start=(k == 0), stop=(k == G - 1))
                mm.then_inc(mod_mm, 1)
                pe.wait_ge(setup_v, 6)
                for i in range(G):
                    for k in range(G):
                        mm = nc.tensor.matmul(ps[:, i, :], wdT[:, k, i * P:(i + 1) * P], wtau[:, k, :],
                                              start=(k == 0), stop=(k == G - 1))
                mm.then_inc(wdt_mm, 1)
                pe.wait_ge(halo_v, 4)
                for g in range(G):
                    mm = nc.tensor.transpose(ps[:, 5, g * NH:(g + 1) * NH], hx[0:NH, g * P:(g + 1) * P], identity[0:NH, 0:NH])
                mm.then_inc(halo_mm, 1)
                pe.wait_ge(halo_v, 4 + 4 * G)
                for m in range(G):
                    for k in range(G):
                        mm = nc.tensor.matmul(ps[:, 6, m * NH:(m + 1) * NH], win_sb[:, k, m * P:(m + 1) * P], hh[:, k, :],
                                              start=(k == 0), stop=(k == G - 1))
                mm.then_inc(halo_mm, 1)

            @block.vector
            def _(dve):
                v = nc.vector
                count = [0]

                def done(ins):
                    count[0] += 1
                    ins.then_inc(setup_v, 1)

                dve.wait_ge(mod_mm, 1)
                for m, add in enumerate((0.0, 1.0, 0.0, 0.0, 1.0, 0.0)):
                    done(v.tensor_scalar(modrow[m][0:NB], ps[0:NB, m, :], add, None, ALU.add))
                dve.wait_ge(setup_v, 6)
                for i, m in enumerate((R_GA, R_GB)):
                    done(v.tensor_scalar(signs[0:NB, i, :], modrow[m][0:NB], 0.0, 2.0, ALU.is_ge, ALU.mult))
                    done(v.scalar_tensor_tensor(mags[0:NB, i, :], modrow[m][0:NB], -1.0, modrow[m][0:NB], ALU.mult, ALU.max))
                dve.wait_ge(setup_v, 10)
                for i in range(2):
                    done(v.tensor_scalar(signs[0:NB, i, :], signs[0:NB, i, :], -1.0, None, ALU.add))
                    done(v.tensor_scalar(mags[0:NB, i, :], mags[0:NB, i, :], 0.25, None, ALU.max))
                dve.wait_ge(setup_v, 14)
                v.tensor_tensor(modrow[R_GB][0:NB], signs[0:NB, 1, :], mags[0:NB, 1, :], ALU.mult).then_inc(rows_v, 1)
                done(v.tensor_tensor(modrow[R_GA][0:NB], signs[0:NB, 0, :], mags[0:NB, 0, :], ALU.mult))
                dve.wait_ge(setup_v, 15)
                v.tensor_tensor(modrow[R_SAGA][0:NB], modrow[0][0:NB], modrow[R_GA][0:NB], ALU.mult).then_inc(rows_v, 1)
                v.tensor_tensor(modrow[R_CAGA][0:NB], modrow[1][0:NB], modrow[R_GA][0:NB], ALU.mult).then_inc(rows_v, 1)
                dve.wait_ge(mod_mm, 2)
                done(v.tensor_copy(tau_bias[:], ps[:, 7, 0:G]))
                dve.wait_ge(a_done, 1)
                done(v.tensor_scalar(negA[:], absA, -1.0, None, ALU.mult))
                done(v.tensor_scalar(halfA[:], absA, -0.5, None, ALU.mult))
                done(v.tensor_scalar(z_scale[:], absA, 1.0 / DA_EPS, None, ALU.mult))
                done(v.memset(consts[:, 0:1], -1.0))
                done(v.memset(consts[:, 1:2], LN_EPS))
                done(v.memset(consts[:, 2:3], 1e-18))
                done(v.memset(carry[:], 0.0))
                dve.wait_ge(setup_v, count[0])
                done(v.reciprocal(recipA[:], negA[:]))
                dve.wait_ge(ld_pads, 64)
                v.bn_stats(stats[0:NH, 0, :], hx[0:NH, :]).then_inc(halo_v, 1)
                dve.wait_ge(halo_v, 1)
                v.bn_aggr(momA[0:NH, 0, :], stats[0:NH, 0, :]).then_inc(halo_v, 1)
                dve.wait_ge(halo_sq, 1)
                v.reciprocal(spreadA[0:NH, 1:2], spreadA[0:NH, 0:1]).then_inc(halo_v, 1)
                dve.wait_ge(halo_v, 3)
                v.tensor_scalar(hx[0:NH, :], hx[0:NH, :], momA[0:NH, 0, 0:1], spreadA[0:NH, 1:2], ALU.subtract,
                                ALU.mult).then_inc(halo_v, 1)
                dve.wait_ge(ld_mod, 32 * G)
                dve.wait_ge(halo_mm, 1)
                n = 4
                for step_, (m, op) in enumerate(((1, ALU.mult), (0, ALU.add))):
                    if step_:
                        dve.wait_ge(halo_v, n)
                    for g in range(G):
                        for side in range(2):
                            dst = hh[:, g, side * NBLK:(side + 1) * NBLK].rearrange("p (b r) -> p b r", r=PER)
                            src = ps[:, 5, g * NH + side * NBLK:g * NH + (side + 1) * NBLK].rearrange("p (b r) -> p b r", r=PER)
                            v.tensor_tensor(dst, dst if step_ else src,
                                            modh[:, m, g, :].unsqueeze(2).broadcast_to([P, NB, PER]), op).then_inc(halo_v, 1)
                            n += 1
                dve.wait_ge(halo_mm, 2)
                v.tensor_copy(flat(halo[:]), ps[:, 6, 0:G * NH]).then_inc(halo_v, 1)
                dve.wait_ge(halo_v, n + 1)
                v.memset(halo[:, :, 0:NBLK:PER], 0.0)
                v.memset(halo[:, :, NBLK + PER - 1:NH:PER], 0.0).then_inc(halo_v, 1)
                dve.wait_ge(halo_v, n + 2)
                dve.wait_ge(setup_v, count[0])

        z_done, inv_steps, exp_done, factor_steps, factor_done = (
            sem("z_done"), sem("inv_steps"), sem("exp_done"), sem("factor_steps"), sem("factor_done"))
        w_done, bu_done, scan_done, carry_done, hC_done = (
            sem("uB_done"), sem("bu_done"), sem("scan_done"), sem("carry_done"), sem("hC_done"))
        B_ready, C_ready, y_summed, y_taken = sem("B_ready"), sem("C_ready"), sem("y_summed"), sem("y_taken")
        delta_moved, u_moved, bc_moved = sem("delta_moved"), sem("u_moved"), sem("bc_moved")
        a_ld, a_stat, a_sqrt, a_rstd, a_xn, a_job, a_aev, a_edge, a_v, a_conv, a_silu = (
            sem("a_loaded"), sem("a_stats"), sem("a_sqrt"), sem("a_rstd"), sem("a_normalized"), sem("a_jobs"),
            sem("a_evicted"), sem("a_edges"), sem("a_conv_steps"), sem("a_conv"), sem("a_silu"))
        a_e, a_corr, a_ln, a_diff, a_delta, a_bc = (
            sem("a_exp_steps"), sem("a_correction_steps"), sem("a_ln"), sem("a_log1p"), sem("a_delta"), sem("a_bc_steps"))
        f_ld, f_gb, f_xn, f_job, f_aev, f_dev, f_gated, f_res, f_stat, f_sqrt, f_rstd, f_xn2 = (
            sem("f_loaded"), sem("f_gb_loaded"), sem("f_normalized"), sem("f_jobs"), sem("f_evicted_act"),
            sem("f_evicted_dve"), sem("f_gated"), sem("f_resid_steps"), sem("f_stats"), sem("f_sqrt"), sem("f_rstd"),
            sem("f_normalized2"))
        f_top, f_gates, f_wl, f_fin, f_out, f_st = (
            sem("f_top_steps"), sem("f_gates"), [sem("expert_loaded_0"), sem("expert_loaded_1")], sem("f_final"),
            sem("f_out_done"), sem("f_stored"))

        JA_T, JA_VAL, JA_P, JA_BC, JA = 0, G, 2 * G, 3 * G, 3 * G + 1
        JF_T, JF_GATE, JF_OUT, JF_T2, JF_LOG, JF_W1_0 = 0, G, 2 * G, 2 * G + TPB, 3 * G + TPB, 3 * G + TPB + 1
        JF = 3 * G + TPB + 1 + 1 + EX * (HT + TPB)
        AEV_F = 3 * G + 1 + EX * HT
        DEV_F = TPB + 1 + EX * TPB

        def aev_gelu(e):
            return 3 * G + 1 + e * HT

        def dev_w2(e):
            return TPB + e * TPB + (e > 0)

        DEV_GT = 2 * TPB

        def f_job_no(what, e=0):
            order = [("t", 0)] * G + [("gate", 0)] * G + [("out", 0)] * TPB + [("t2", 0)] * G + [("log", 0)]
            order += [("w1", 0)] * HT
            for i in range(E):
                order += [("w2", i)] * TPB + [("w1", i + 1)] * HT
                if i == 0:
                    order += [("gT", 0)]
            order += [("w2", E)] * TPB
            assert len(order) == JF
            return order.index((what, e))

        SLOT_W2 = N - EX

        def sync_block(sp, it, scan, A, F):
            a, f = it + 1, it - 1
            kp = "(k p) n -> p k n"

            def load_w1(e):
                sp.dma_start(w1_e[:, e % 2], W1[:, e * HID:(e + 1) * HID].rearrange(kp, p=P)).then_inc(f_wl[e % 2], 16)

            def load_w2(e):
                sp.dma_start(w2_e[:, e % 2], W2[e * HID:(e + 1) * HID, :].rearrange(kp, p=P)).then_inc(f_wl[e % 2], 16)

            if F:
                sp.wait_ge(f_out, f + 1)
                load_w1(0)
                block_f = f * T if isinstance(f, int) else sp.snap(f * T)
                row = h_rows[bass.ds(f, 1), :]
                sp.dma_start(x1[:], x_flat[bass.ds(block_f, T), :].rearrange("(t p) d -> p t d", p=P)).then_inc(f_ld, 16)
                for i, m in enumerate((R_SAGA, R_CAGA, R_GA)):
                    sp.dma_start(rows[:, i, :], row[:, m * D:(m + 1) * D].partition_broadcast(P)
                                 .rearrange("p o d -> p (o d)")).then_inc(f_ld, 16)
                sp.dma_start(modF[:], row[:, 0:5 * D].rearrange("o (m g p) -> p (o m) g", m=5, p=P)).then_inc(f_ld, 16)
                load_w2(0)
            if A:
                ge(sp, u_moved, it + 1)
                ge(sp, w_done, it * N + 1 if scan else 0)
                ge(sp, a_aev, (a - 1) * (3 * G) + G)
            if F:
                load_w1(1)
            if A:
                sp.dma_start(xa, x_flat[bass.ds(a * T, T), :].rearrange("(t p) d -> p t d", p=P)).then_inc(a_ld, 16)
                sp.dma_start(modA[:], h_rows[bass.ds(a, 1), 0:5 * D].rearrange("o (m g p) -> p (o m) g", m=5, p=P)).then_inc(a_ld, 16)
            if F:
                load_w2(1)
                for e in range(2, EX):
                    if e == 2:
                        sp.wait_ge(f_dev, f * DEV_F + 1 + TPB)
                    sp.wait_ge(f_job, f * JF + f_job_no("w2", e - 2) + TPB)
                    load_w1(e)
                    load_w2(e)
                    if e == 2:
                        sp.dma_start(rows[:, 2, :], h_rows[bass.ds(f, 1), R_GB * D:(R_GB + 1) * D].partition_broadcast(P)
                                     .rearrange("p o d -> p (o d)")).then_inc(f_gb, 16)
                sp.wait_ge(f_out, f + 2)
                sp.dma_start(out_flat[bass.ds(block_f, T), :].rearrange("(t p) d -> p t d", p=P), xn[:]).then_inc(f_st, 16)

        def act_block(act, it, scan, A, F, prev):
            s = nc.scalar
            a, f = it + 1, it - 1

            def evict(kind, dst, bank, func, **kw):
                s.activation(dst, ps[:, bank, :], func, **kw).then_inc(a_aev if kind == "A" else f_aev, 1)

            def chain(n):
                c = it * N + n
                nn = n % N
                p = nn % 2
                d = delta_next if n == N else delta
                ge(act, z_done, c + 1)
                ge(act, scan_done, c - 1)
                s.activation(inv[:, p], zq[:], ACT.Square, bias=consts[:, 0:1]).then_inc(inv_steps, 1)
                ge(act, inv_steps, 3 * c + 1)
                s.activation(inv[:, p], inv[:, p], ACT.Ln, bias=consts[:, 2:3]).then_inc(inv_steps, 1)
                ge(act, inv_steps, 3 * c + 2)
                s.activation(inv[:, p], inv[:, p], ACT.Exp, scale=-1.0).then_inc(inv_steps, 1)
                if n == N:
                    ge(act, a_delta, it + 2)
                elif n == 1:
                    ge(act, delta_moved, it + 1)
                for g in range(G):
                    s.activation(th[:, p, g, :], d[:, g, :], ACT.Tanh, scale=halfA[:, nn, g:g + 1])
                for g in range(G):
                    ins = s.activation(abar[:, p, g, :], d[:, g, :], ACT.Exp, scale=negA[:, nn, g:g + 1])
                ins.then_inc(exp_done, 1)

            for slot in range(N):
                if scan and slot + 1 < N:
                    chain(slot + 1)
                elif A and slot + 1 == N:
                    chain(N)
                    s.activation(delta[:], delta_next[:], ACT.Identity).then_inc(delta_moved, 1)
                    ge(act, w_done, it * N + N)
                    act.wait_ge(a_silu, a + 1)
                    s.activation(u[:], u_next[:], ACT.Identity).then_inc(u_moved, 1)
                if prev and slot == 0:
                    ge(act, y_summed, it * N)
                    ge(act, a_diff, it + 1 if scan else it)
                    s.activation(ys[:], ps[:, Y_BANK:Y_BANK + G, :], ACT.Identity).then_inc(y_taken, 1)
                if F and slot == 0:
                    act.wait_ge(f_ld, f * 80 + 80)
                    for g in range(G):
                        act.wait_ge(f_job, f * JF + JF_T + g + 1)
                        evict("F", hf[:, g, :], bank_F[JF_T + g], ACT.Identity, bias=modF[:, 0, g:g + 1], scale=modF[:, 1, g:g + 1])
                if A and slot == 1:
                    ge(act, a_stat, a * (TPB + 1) + TPB + 1)
                    s.activation(spreadA[:], momA[:, :, 1], ACT.Sqrt, bias=consts[:, 1:2]).then_inc(a_sqrt, 1)
                if F and slot == 1:
                    for g in range(G):
                        act.wait_ge(f_job, f * JF + JF_GATE + g + 1)
                        evict("F", gate[:, g, :], bank_F[JF_GATE + g], ACT.Silu)
                if A and slot == 2:
                    ge(act, a_ld, a * 32 + 32)
                    for g in range(G):
                        act.wait_ge(a_job, a * JA + JA_T + g + 1)
                        evict("A", hT[:, g, :], bank_A[JA_T + g], ACT.Identity, bias=modA[:, 0, g:g + 1], scale=modA[:, 1, g:g + 1])
                if F and slot == 3:
                    act.wait_ge(f_stat, f * (TPB + 1) + TPB + 1)
                    s.activation(spreadF[:], momF[:, :, 1], ACT.Sqrt, bias=consts[:, 1:2]).then_inc(f_sqrt, 1)
                if A and slot == 3:
                    ge(act, a_delta, a)
                    for g in range(G):
                        act.wait_ge(a_job, a * JA + JA_VAL + g + 1)
                        evict("A", valp[:, g, 1:T + 1], bank_A[JA_VAL + g], ACT.Identity)
                if F and slot == 4:
                    for g in range(G):
                        act.wait_ge(f_job, f * JF + JF_T2 + g + 1)
                        evict("F", hf[:, g, :], bank_F[JF_T2 + g], ACT.Identity, bias=modF[:, 3, g:g + 1], scale=modF[:, 4, g:g + 1])
                if A and slot == 5:
                    act.wait_ge(a_conv, a + 1)
                    s.activation(u_next[:], u_next[:], ACT.Silu).then_inc(a_silu, 1)
                if F and slot == 5:
                    act.wait_ge(f_job, f * JF + JF_LOG + 1)
                    s.activation(flat(sco[:]), ps[:, bank_F[JF_LOG], 0:TPB * E], ACT.Sigmoid).then_inc(f_aev, 1)
                if A and slot == 6:
                    for g in range(G):
                        act.wait_ge(a_job, a * JA + JA_P + g + 1)
                        evict("A", delta_next[:, g, :], bank_A[JA_P + g], ACT.Identity, bias=tau_bias[:, g:g + 1])
                    act.wait_ge(a_aev, a * (3 * G) + 3 * G)
                    if F:
                        act.wait_ge(f_job, f * JF + JF_OUT + TPB)
                    s.activation(e_neg[:], delta_next[:], ACT.Abs).then_inc(a_e, 1)
                    act.wait_ge(a_e, a * 2 + 1)
                    s.activation(e_neg[:], e_neg[:], ACT.Exp, scale=-1.0).then_inc(a_e, 1)
                if A and slot == 9:
                    act.wait_ge(a_corr, a * 2 + 2)
                    s.activation(lnw, lnw, ACT.Ln).then_inc(a_ln, 1)
                if F and (slot == 5 or SLOT_W2 <= slot < N - 1):
                    e = 0 if slot == 5 else slot - SLOT_W2 + 1
                    if e >= 2:
                        act.wait_ge(f_job, f * JF + f_job_no("w2", e - 2) + TPB)
                    elif e == 0:
                        act.wait_ge(f_gated, f + 1)
                    for h in range(HT):
                        act.wait_ge(f_job, f * JF + f_job_no("w1", e) + h + 1)
                        evict("F", hid[:, e % 2, h, :], bank_F[f_job_no("w1", e) + h], ACT.Gelu,
                              bias=b1_sb[:, e * HT + h:e * HT + h + 1])

        def pe_slots(A, F):
            early = {s_: [] for s_ in range(N)}
            late = {s_: [] for s_ in range(N)}
            if F:
                late[0] += [("F", "t", 0, g) for g in range(G)]
                early[1] += [("F", "gate", 0, g) for g in range(G)]
                early[2] += [("F", "out", 0, t_) for t_ in range(TPB)]
            if A:
                late[2] += [("A", "t", 0, g) for g in range(G)]
                early[3] += [("A", "val", 0, g) for g in range(G)]
            if F:
                early[4] += [("F", "t2", 0, g) for g in range(G)]
                early[5] += [("F", "log", 0, 0)] + [("F", "w1", 0, h) for h in range(HT)]
            if A:
                early[6] += [("A", "p", 0, g) for g in range(G)]
            if F:
                for e in range(EX):
                    early[SLOT_W2 + e] += [("F", "w2", e, t_) for t_ in range(TPB)]
                    if e + 1 < EX:
                        early[SLOT_W2 + e] += [("F", "w1", e + 1, h) for h in range(HT)]
                late[SLOT_W2] += [("F", "gT", 0, 0)]
            if A:
                late[8] += [("A", "bc", 0, 0)]
            return early, late

        def plan_banks(A, F):
            early, late = pe_slots(A, F)
            plan, last, n, nA, nF = {}, {}, 0, 0, 0
            for s_ in range(N):
                for job in early[s_] + late[s_]:
                    bank = JOB_BANK + n % 2
                    no = nA if job[0] == "A" else nF
                    plan[(job[0], no)] = (bank, last.get(bank))
                    last[bank] = (job, no)
                    n += 1
                    nA += job[0] == "A"
                    nF += job[0] == "F"
            return plan, last

        def evicted(job, no, a, f):
            kind, what, e, i = job
            if kind == "A":
                return (a_bc, a * 6 + 2) if what == "bc" else (a_aev, a * (3 * G) + no + 1)
            if what in ("out", "gT", "w2"):
                return f_dev, f * DEV_F + 1 + {"out": i, "gT": DEV_GT, "w2": dev_w2(e) + i}[what] + 1
            return f_aev, f * AEV_F + {"t": i, "gate": G + i, "t2": 2 * G + i, "log": 3 * G, "w1": aev_gelu(e) + i}[what] + 1

        def pe_block(pe, it, scan, A, F, prev, plan):
            t = nc.tensor
            a, f = it + 1, it - 1
            early, late = pe_slots(A, F)
            numbers = {"A": 0, "F": 0}

            def job(kind, what, e, i):
                no = numbers[kind]
                numbers[kind] += 1
                bank, before = plan[(kind, no)]
                if before is not None:
                    sm, val = evicted(before[0], before[1], a, f)
                    ge(pe, sm, val)
                elif F:
                    pe.wait_ge(f_dev, f * DEV_F + 1)
                o = ps[:, bank, :]
                if what == "t":
                    src = xa if kind == "A" else xn
                    if i == 0:
                        pe.wait_ge(a_xn if kind == "A" else f_xn, (a if kind == "A" else f) + 1)
                    for tt in range(TPB):
                        mm = t.transpose(o[:, tt * P:(tt + 1) * P], src[:, tt, i * P:(i + 1) * P], identity[:])
                elif what == "val" or what == "gate":
                    if i == 0:
                        pe.wait_ge(a_aev if kind == "A" else f_aev, (a * (3 * G) if kind == "A" else f * AEV_F) + G)
                    m = i + (G if what == "gate" else 0)
                    h = hT if kind == "A" else hf
                    for k in range(G):
                        mm = t.matmul(o, win_sb[:, k, m * P:(m + 1) * P], h[:, k, :], start=(k == 0), stop=(k == G - 1))
                elif what == "p":
                    if i == 0:
                        pe.wait_ge(a_silu, a + 1)
                    for k in range(G):
                        mm = t.matmul(o, wdt_sb[:, k, i * P:(i + 1) * P], u_next[:, k, :], start=(k == 0), stop=(k == G - 1))
                elif what == "bc":
                    for k in range(G):
                        mm = t.matmul(o[0:2 * N, :], wbc_sb[:, k, :], u_next[:, k, :], start=(k == 0), stop=(k == G - 1))
                elif what == "out":
                    if i == 0:
                        pe.wait_ge(f_gated, f + 1)
                    for k in range(G):
                        mm = t.matmul(o, ys[:, k, i * P:(i + 1) * P], wout_sb[:, k, :], start=(k == 0), stop=(k == G - 1))
                elif what == "t2":
                    if i == 0:
                        pe.wait_ge(f_xn2, f + 1)
                    for tt in range(TPB):
                        mm = t.transpose(o[:, tt * P:(tt + 1) * P], xn[:, tt, i * P:(i + 1) * P], identity[:])
                elif what == "log":
                    pe.wait_ge(f_aev, f * AEV_F + 3 * G)
                    for tt in range(TPB):
                        for k in range(G):
                            mm = t.matmul(o[:, tt * E:(tt + 1) * E], hf[:, k, tt * P:(tt + 1) * P], gw_sb[:, k, :],
                                          start=(k == 0), stop=(k == G - 1))
                elif what == "w1":
                    if i == 0:
                        pe.wait_ge(f_wl[e % 2], f * (32 * ((EX + 1 - e % 2) // 2)) + 32 * (e // 2 + 1))
                    for k in range(G):
                        mm = t.matmul(o, w1_e[:, e % 2, k, i * P:(i + 1) * P], hf[:, k, :], start=(k == 0), stop=(k == G - 1))
                elif what == "gT":
                    pe.wait_ge(f_gates, f + 1)
                    for tt in range(TPB):
                        mm = t.transpose(o[0:EX, tt * P:(tt + 1) * P], gates[:, tt, :], identity[:])
                elif what == "w2":
                    if i == 0:
                        pe.wait_ge(f_aev, f * AEV_F + aev_gelu(e) + HT)
                    if e == E:
                        if i == 0:
                            pe.wait_ge(f_dev, f * DEV_F + 1 + DEV_GT + 1)
                        t.matmul(o, gT[0:EX, i * P:(i + 1) * P], b2_sb[:, :], start=True, stop=False)
                    for h in range(HT):
                        mm = t.matmul(o, hid[:, e % 2, h, i * P:(i + 1) * P], w2_e[:, e % 2, h, :],
                                      start=(h == 0 and e < E), stop=(h == HT - 1))
                mm.then_inc(a_job if kind == "A" else f_job, 1)

            def spread(bank, n, src, ready):
                t.matmul(ps[:, bank, :], pick[:, n:n + 1].broadcast_to([3 * 2 * N, P]), src[:, :], start=True,
                         stop=True).then_inc(ready, 1)

            def sum_y(n, c):
                ge(pe, hC_done, c)
                if n == 0:
                    ge(pe, y_taken, it)
                for g in range(G):
                    mm = t.matmul(ps[:, Y_BANK + g, :], identity[:], hs[:, g, :], start=(n == 0), stop=(n == N - 1),
                                  skip_group_check=True)
                mm.then_inc(y_summed, 1)

            for slot in range(N):
                if slot == 0 and prev:
                    sum_y(N - 1, it * N)
                elif slot and scan:
                    sum_y(slot - 1, it * N + slot)
                if scan:
                    if slot == 0:
                        pe.wait_ge(bc_moved, it + 1)
                        ge(pe, hC_done, it * N)
                    spread(C_BANK, N + slot, BC3, C_ready)
                for j in early[slot]:
                    job(*j)
                if scan and slot + 1 < N:
                    pe.wait_ge(w_done, it * N + slot + 1)
                    spread(B_BANK, slot + 1, BC3, B_ready)
                elif A and slot + 1 == N:
                    ge(pe, w_done, it * N + N)
                    pe.wait_ge(a_bc, a * 6 + 6)
                    spread(B_BANK, 0, BC3_next, B_ready)
                for j in late[slot]:
                    job(*j)

        def dve_block(dve, it, scan, A, F):
            v = nc.vector
            a, f = it + 1, it - 1

            def make_z(n):
                src = delta_next if n == N else delta
                if n == N:
                    dve.wait_ge(a_delta, a + 1)
                elif n == 1:
                    dve.wait_ge(delta_moved, it + 1)
                for g in range(G):
                    ins = v.tensor_scalar(zq[:, g, :], src[:, g, :], z_scale[:, n % N, g:g + 1], Z_CAP, ALU.mult, ALU.min)
                ins.then_inc(z_done, 1)

            def w2_sum(e, tt):
                dve.wait_ge(f_job, f * JF + f_job_no("w2", e) + tt + 1)
                src = ps[:, bank_F[f_job_no("w2", e) + tt], :]
                if e == 0:
                    dve.wait_ge(f_gates, f + 1)
                    ins = v.tensor_scalar(xn[:, tt, :], src, gates[:, tt, 0:1], None, ALU.mult)
                else:
                    dve.wait_ge(f_dev, f * DEV_F + 1 + dev_w2(e - 1) + tt + 1)
                    ins = v.scalar_tensor_tensor(xn[:, tt, :], src, gates[:, tt, e:e + 1], xn[:, tt, :], ALU.mult, ALU.add)
                ins.then_inc(f_dev, 1)

            def normalize_f1():
                dve.wait_ge(f_ld, f * 80 + 80)
                dve.wait_ge(f_st, f * 16 + 1)
                for tt in range(TPB):
                    nm = norms[:, bass.ds(f, 1), tt, :]
                    ins = v.tensor_scalar(xn[:, tt, :], x1[:, tt, :], nm[:, :, 0], nm[:, :, 1], ALU.subtract, ALU.mult)
                ins.then_inc(f_xn, 1)

            def stats_of(src, st, mom, sm, base_):
                for tt in range(TPB):
                    v.bn_stats(st[:, tt, :], src[:, tt, :]).then_inc(sm, 1)
                dve.wait_ge(sm, base_ + TPB)
                v.memset(gates[:, :, E:EX], 1.0)
                for tt in range(TPB):
                    ins = v.bn_aggr(mom[:, tt, :], st[:, tt, :])
                ins.then_inc(sm, 1)

            def stats_A():
                dve.wait_ge(a_ld, a * 32 + 32)
                stats_of(xa, stats, momA, a_stat, a * (TPB + 1))

            def normalize_A():
                dve.wait_ge(a_sqrt, a + 1)
                v.reciprocal(spreadA[:], spreadA[:]).then_inc(a_rstd, 1)
                dve.wait_ge(a_rstd, a + 1)
                for tt in range(TPB):
                    ins = v.tensor_scalar(xa[:, tt, :], xa[:, tt, :], momA[:, tt, 0:1], spreadA[:, tt:tt + 1],
                                          ALU.subtract, ALU.mult)
                ins.then_inc(a_xn, 1)
                nm = norms[:, bass.ds(a, 1), :, :].rearrange("p o t s -> p (o t) s")
                v.tensor_copy(nm[:, :, 0], momA[:, :, 0])
                v.tensor_copy(nm[:, :, 1], spreadA[:])

            def resid_before():
                dve.wait_ge(f_job, f * JF + JF_T + G)
                v.tensor_tensor(x1[:], x1[:], rows[:, 0, :].unsqueeze(1).broadcast_to([P, TPB, D]), ALU.add).then_inc(f_res, 1)
                v.tensor_tensor(xn[:], xn[:], rows[:, 1, :].unsqueeze(1).broadcast_to([P, TPB, D]), ALU.mult).then_inc(f_res, 1)
                dve.wait_ge(f_res, f * 4 + 2)
                v.tensor_tensor(x1[:], x1[:], xn[:], ALU.add).then_inc(f_res, 1)

            def gated():
                dve.wait_ge(y_taken, it)
                dve.wait_ge(f_aev, f * AEV_F + 2 * G)
                v.tensor_tensor(ys[:], ys[:], gate, ALU.mult).then_inc(f_gated, 1)

            def take_out(tt):
                dve.wait_ge(f_job, f * JF + JF_OUT + tt + 1)
                v.tensor_tensor(og[:, tt, :], ps[:, bank_F[JF_OUT + tt], :], rows[:, 2, :], ALU.mult).then_inc(f_dev, 1)

            def resid_after():
                dve.wait_ge(f_dev, f * DEV_F + 1 + TPB)
                dve.wait_ge(f_res, f * 4 + 3)
                v.tensor_tensor(x1[:], x1[:], og, ALU.add).then_inc(f_res, 1)
                dve.wait_ge(f_res, f * 4 + 4)
                stats_of(x1, statsF, momF, f_stat, f * (TPB + 1))

            def normalize_f2():
                dve.wait_ge(f_sqrt, f + 1)
                v.reciprocal(rstdF[:], spreadF[:]).then_inc(f_rstd, 1)
                dve.wait_ge(f_rstd, f + 1)
                for tt in range(TPB):
                    ins = v.tensor_scalar(xn[:, tt, :], x1[:, tt, :], momF[:, tt, 0:1], rstdF[:, tt:tt + 1],
                                          ALU.subtract, ALU.mult)
                ins.then_inc(f_xn2, 1)

            def conv():
                dve.wait_ge(a_aev, a * (3 * G) + 2 * G)
                v.tensor_copy(valp[:, :, 0:1], halo[:, :, bass.ds(a, 1)])
                v.tensor_copy(valp[:, :, T + 1:T + 2], halo[:, :, bass.ds(a + NBLK, 1)]).then_inc(a_edge, 1)
                dve.wait_ge(a_edge, a + 1)
                for g in range(G):
                    ins = v.tensor_scalar(u_next[:, g, :], valp[:, g, 0:T], conv_taps[:, g, 0:1], None, ALU.mult)
                ins.then_inc(a_v, 1)
                for tap in (1, 2):
                    dve.wait_ge(a_v, a * 2 + tap)
                    for g in range(G):
                        ins = v.scalar_tensor_tensor(u_next[:, g, :], valp[:, g, tap:T + tap], conv_taps[:, g, tap:tap + 1],
                                                     u_next[:, g, :], ALU.mult, ALU.add)
                    ins.then_inc(a_v if tap == 1 else a_conv, 1)

            def top_two():
                n = [0]

                def step(ins):
                    n[0] += 1
                    ins.then_inc(f_top, 1)
                    dve.wait_ge(f_top, f * 8 + n[0])

                dve.wait_ge(f_aev, f * AEV_F + 3 * G + 1)
                step(v.tensor_scalar(sco[:], sco[:], rs_sb[:, 0:1], None, ALU.mult))
                other = sco[:].unsqueeze(2).broadcast_to([P, TPB, E, E])
                mine = sco[:].unsqueeze(3).broadcast_to([P, TPB, E, E])
                v.tensor_tensor(above, other, mine, ALU.is_gt)
                step(v.tensor_tensor(ties, other, mine, ALU.is_equal))
                step(v.tensor_tensor(ties, ties, low[:].unsqueeze(1).broadcast_to([P, TPB, E, E]), ALU.mult))
                step(v.tensor_tensor(above, above, ties, ALU.add))
                step(v.tensor_reduce(rank[:], above, AX_X, ALU.add))
                step(v.scalar_tensor_tensor(gates[:, :, 0:E], rank[:], 1.5, sco[:], ALU.is_lt, ALU.mult))
                step(v.tensor_reduce(gsum[:], gates[:, :, 0:E], AX_X, ALU.add))
                step(v.reciprocal(gsum[:], gsum[:]))
                assert n[0] == 8
                v.tensor_tensor(gates[:, :, 0:E], gates[:, :, 0:E], gsum[:].unsqueeze(2).broadcast_to([P, TPB, E]),
                                ALU.mult).then_inc(f_gates, 1)

            def take_gT():
                no = f_job_no("gT")
                dve.wait_ge(f_job, f * JF + no + 1)
                v.tensor_copy(gT[0:EX, :], ps[0:EX, bank_F[no], :]).then_inc(f_dev, 1)

            def softplus_correction():
                dve.wait_ge(a_e, a * 2 + 2)
                v.tensor_scalar(lnw, e_neg[:], 1.0, None, ALU.add).then_inc(a_corr, 1)
                dve.wait_ge(a_corr, a * 2 + 1)
                v.scalar_tensor_tensor(e_neg[:], lnw, -1.0, e_neg[:], ALU.add, ALU.subtract).then_inc(a_corr, 1)

            def softplus_end():
                dve.wait_ge(a_ln, a + 1)
                v.tensor_tensor(lnw, lnw, e_neg[:], ALU.subtract).then_inc(a_diff, 1)
                dve.wait_ge(a_diff, a + 1)
                v.scalar_tensor_tensor(delta_next[:], delta_next[:], 0.0, lnw, ALU.max, ALU.add).then_inc(a_delta, 1)

            def split_bc():
                def own(k):
                    dve.wait_ge(a_bc, a * 6 + k)

                src = ps[0:2 * N, bank_A[JA_BC], :]
                dve.wait_ge(a_job, a * JA + JA)
                v.tensor_copy(BC3_next[0:2 * N, :], src).then_inc(a_bc, 1)
                own(1)
                v.tensor_tensor(split[:, 0, :], src, BC3_next[0:2 * N, :], ALU.subtract).then_inc(a_bc, 1)
                own(2)
                v.tensor_copy(mid16, split[:, 0, :]).then_inc(a_bc, 1)
                own(3)
                v.tensor_tensor(split[:, 1, :], split[:, 0, :], mid16, ALU.subtract).then_inc(a_bc, 1)
                own(4)
                v.tensor_copy(BC3_next[2 * N:4 * N, :], mid16).then_inc(a_bc, 1)
                v.tensor_copy(BC3_next[4 * N:6 * N, :], split[:, 1, :]).then_inc(a_bc, 1)
                own(6)

            def finish_block():
                dve.wait_ge(f_gb, f * 16 + 16)
                dve.wait_ge(f_dev, f * DEV_F + 1 + DEV_F)
                v.tensor_tensor(xn[:], xn[:], rows[:, 2, :].unsqueeze(1).broadcast_to([P, TPB, D]), ALU.mult).then_inc(f_fin, 1)
                dve.wait_ge(f_fin, f + 1)
                v.tensor_tensor(xn[:], xn[:], x1[:], ALU.add).then_inc(f_out, 1)

            def background(slot, place):
                if F:
                    if slot == 0 and place == 5:
                        normalize_f1()
                    if slot == 1 and place == 5:
                        resid_before()
                    if slot == 2 and place == 1:
                        gated()
                    if slot == 2 and place in (4, 5):
                        take_out(place - 4)
                    if slot == 3 and place in (0, 1):
                        take_out(place + 2)
                        if place == 1:
                            resid_after()
                    if slot == 4 and place == 0:
                        normalize_f2()
                    if slot == 6 and place == 1:
                        top_two()
                    if slot == 8 and place == 0:
                        take_gT()
                    if slot >= SLOT_W2 and place in (2, 3, 4, 5):
                        w2_sum(slot - SLOT_W2, place - 2)
                    if slot == N - 1 and place == 5:
                        finish_block()
                if A:
                    if slot == 0 and place == 5:
                        stats_A()
                    if slot == 2 and place == 1:
                        normalize_A()
                    if slot == 4 and place == 5:
                        conv()
                    if slot == 8 and place == 5:
                        softplus_correction()
                    if slot == 9 and place == 1:
                        split_bc()
                    if slot == 10 and place == 5:
                        softplus_end()

            for n in range(N):
                p = n % 2
                c = it * N + n
                background(n, 0)
                if scan:
                    dve.wait_ge(inv_steps, 3 * c + 3)
                    dve.wait_ge(z_done, c + 1)
                    v.scalar_tensor_tensor(inv[:, p], zq[:], -1.0, inv[:, p], ALU.add, ALU.mult).then_inc(factor_steps, 1)
                    dve.wait_ge(exp_done, c + 1)
                    v.scalar_tensor_tensor(th[:, p], abar[:, p], 1.0, th[:, p], ALU.add, ALU.mult).then_inc(factor_steps, 1)
                    dve.wait_ge(factor_steps, 2 * c + 2)
                    v.scalar_tensor_tensor(th[:, p], inv[:, p], 1.0, th[:, p], ALU.add, ALU.mult).then_inc(factor_done, 1)
                background(n, 1)
                if (scan and n + 1 < N) or (A and n + 1 == N):
                    make_z(n + 1)
                if scan:
                    dve.wait_ge(B_ready, c + 1)
                    dve.wait_ge(factor_done, c + 1)
                    if n == 1:
                        dve.wait_ge(u_moved, it + 1)
                    uu = u_next if n == 0 else u
                    for g in range(G):
                        ins = v.scalar_tensor_tensor(inv[:, p, g, :], uu[:, g, :], recipA[:, n, g:g + 1],
                                                     ps[:, B_BANK, :], ALU.mult, ALU.mult)
                    ins.then_inc(w_done, 1)
                background(n, 2)
                if scan:
                    dve.wait_ge(w_done, c + 1)
                    v.tensor_tensor(inv[:, p], inv[:, p], th[:, p], ALU.mult).then_inc(bu_done, 1)
                background(n, 3)
                if scan:
                    ge(dve, y_summed, c)
                    ge(dve, carry_done, it * (N + 1))
                    dve.wait_ge(bu_done, c + 1)
                    for g in range(G):
                        ins = v.tensor_tensor_scan(hs[:, g, :], abar[:, p, g, :], inv[:, p, g, :], carry[:, n, g:g + 1],
                                                   ALU.mult, ALU.add)
                    ins.then_inc(scan_done, 1)
                if scan:
                    dve.wait_ge(scan_done, c + 1)
                    v.tensor_copy(carry[:, n, :], hs[:, :, T - 1]).then_inc(carry_done, 1)
                background(n, 4)
                if scan:
                    dve.wait_ge(C_ready, c + 1)
                    dve.wait_ge(carry_done, it * (N + 1) + n + 1)
                    v.tensor_tensor(hs[:], hs[:], ps[:, C_BANK:C_BANK + 1, :].broadcast_to([P, G, T]), ALU.mult).then_inc(hC_done, 1)
                background(n, 5)
            if scan and A:
                dve.wait_ge(carry_done, it * (N + 1) + N)
                v.tensor_scalar(carry[:], carry[:], keep_lim[:, 0, bass.ds(a, 1)], keep_lim[:, 1, bass.ds(a, 1)],
                                ALU.min, ALU.max).then_inc(carry_done, 1)
            if A:
                ge(dve, C_ready, it * N + N)
                dve.wait_ge(a_bc, a * 6 + 6)
                v.tensor_copy(BC3[:], BC3_next[:]).then_inc(bc_moved, 1)

        plans = {key: plan_banks(*key)[0] for key in ((True, True), (True, False), (False, True))}
        bank_A, bank_F = {}, {}

        def use(A, F):
            plan = plans[(A, F)]
            bank_A.clear()
            bank_F.clear()
            for (kind, no), (bank, _) in plan.items():
                (bank_A if kind == "A" else bank_F)[no] = bank
            return plan

        def steps(emit, loop):
            emit(-1, False, True, False, False)
            emit(0, True, True, False, False)
            with loop(1, NBLK - 1) as it:
                emit(it, True, True, True, True)
            emit(NBLK - 1, True, False, True, True)
            emit(NBLK, False, False, True, True)

        with nc.Block() as block:
            @block.sync
            def _(sp):
                steps(lambda it, scan, A, F, prev: sync_block(sp, it, scan, A, F), sp.Fori)
                sp.wait_ge(f_st, 16 * NBLK + 1)

            @block.scalar
            def _(act):
                def emit(it, scan, A, F, prev):
                    use(A, F)
                    act_block(act, it, scan, A, F, prev)
                steps(emit, act.Fori)

            @block.tensor
            def _(pe):
                def emit(it, scan, A, F, prev):
                    pe_block(pe, it, scan, A, F, prev, use(A, F))
                steps(emit, pe.Fori)

            @block.vector
            def _(dve):
                nc.vector.memset(gsum[:, 0:1], 0.0).then_inc(f_out, 1)
                nc.vector.memset(gsum[:, 1:2], 0.0).then_inc(f_st, 1)
                nc.vector.memset(gsum[:, 2:3], 0.0).then_inc(f_dev, 1)

                def emit(it, scan, A, F, prev):
                    use(A, F)
                    dve_block(dve, it, scan, A, F)
                steps(emit, dve.Fori)


def kernel(**inputs):
    import numpy as _np
    import concourse.bacc as _bacc
    from concourse import mybir as _mybir
    from concourse.bass_utils import run_bass_kernel_spmd as _run

    a = {k: _np.asarray(v) for k, v in inputs.items()}
    NB, L, D = a["L0_attn_x"].shape
    N = a["L0_attn_A_log"].shape[1]
    E, _, H = a["L0_ffn_W1"].shape
    c = _np.ascontiguousarray
    laid = {
        "x": a["L0_attn_x"],
        "W_in": a["L0_attn_W_in"],
        "conv_w": a["L0_attn_conv_w"][:, 0, :],
        "W_BC": _np.concatenate([a["L0_attn_W_B"], a["L0_attn_W_C"]], axis=1),
        "W_deltaT": a["L0_attn_W_delta"].T,
        "delta_base": a["L0_attn_delta_base"],
        "W_tau": a["L0_attn_W_tau"],
        "A_log": a["L0_attn_A_log"],
        "W_out": a["L0_attn_W_out"],
        "gate_W": a["L0_ffn_gate_W"],
        "W1": _np.concatenate([a["L0_ffn_W1"].transpose(1, 0, 2).reshape(D, E * H), a["L0_ffn_Ws1"]], axis=1),
        "b1": _np.concatenate([a["L0_ffn_b1"].reshape(E * H), a["L0_ffn_bs1"]]),
        "W2": _np.concatenate([a["L0_ffn_W2"].reshape(E * H, D), a["L0_ffn_Ws2"]], axis=0),
        "b2": _np.concatenate([a["L0_ffn_b2"], a["L0_ffn_bs2"][None, :]], axis=0),
        "route_scale": a["L0_ffn_route_scale"].reshape(1),
        "cT": a["L0_c"].T,
        "wmod": a["L0_wmod"],
        "ident": _np.eye(128, dtype=_np.float32),
        "onehot": _np.tile(_np.eye(2 * N, dtype=_np.float32), (3, 1)).astype(_mybir.dt.np(_mybir.dt.bfloat16)),
        "earlier": _np.tril(_np.ones((E, E), _np.float32), -1).reshape(E * E),
        "keep": _np.array([s * (0.0 if i % (L // 512) == 0 else float(_np.finfo(_np.float32).max)) for s in (1, -1) for i in range(NB * L // 512)],
                          _np.float32),
    }
    nc = _bacc.Bacc("TRN2", target_bir_lowering=False, num_devices=1)
    arrays, args = {}, []
    for name, arr in laid.items():
        arr = c(arr)
        arrays[f"in_{name}"] = arr
        args.append(nc.dram_tensor(f"in_{name}", arr.shape, _mybir.dt.from_np(arr.dtype), kind="ExternalInput").ap())
    args.append(nc.dram_tensor("out_0", a["L0_attn_x"].shape, _mybir.dt.float32, kind="ExternalOutput").ap())
    adaln_mamba_moe(nc, *args)
    r = _run(nc, [arrays], core_ids=[0])
    return r.results[0]["out_0"]
```

```python
from contextlib import ExitStack

import numpy as np
import concourse.bass as bass
from concourse import mybir

ALU = mybir.AluOpType
ACT = mybir.ActivationFunctionType
F32 = mybir.dt.float32
BF16 = mybir.dt.bfloat16
AX_X = mybir.AxisListType.X

P = 128
BANK = 512
LN_EPS = 1e-5
DA_EPS = float(np.float32(1e-6))
DELTA_HI = 1e18
Y_CAP = 4e9


def adaln_mamba_moe(nc, x, W_in, conv_w, W_BC, W_deltaT, delta_base, W_tau, A_log, W_out, gate_W, W1, b1, W2, b2,
                    route_scale, cT, wmod, ident, onehot, earlier, keep, out):
    NB, L, D = x.shape
    G = D // P
    N = A_log.shape[1]
    T = BANK
    TPB = T // P
    NBLK = NB * L // T
    PER = L // T
    E = gate_W.shape[1]
    EX = E + 1
    HID = W1.shape[1] // EX
    HT = HID // P
    MODS = wmod.shape[1] // D
    R_GA, R_GB = 2, 5

    h_rows = nc.dram_tensor("row_scratch", [NBLK, MODS * D], F32).ap()
    x_flat = x.rearrange("b l d -> (b l) d")
    out_flat = out.rearrange("b l d -> (b l) d")

    with ExitStack() as ctx:
        ctx.enter_context(nc.allow_non_contiguous_dma(reason="small per-channel tables"))

        def sb(name, shape, dt=F32):
            return ctx.enter_context(nc.sbuf_tensor(name, shape, dt))

        def sem(name):
            return ctx.enter_context(nc.semaphore(name))

        def ge(eng, s, value):
            if not isinstance(value, int) or value > 0:
                eng.wait_ge(s, value)

        ps = ctx.enter_context(nc.psum_tensor("ps", [P, 8, BANK], F32))
        Y_BANK, B_BANK, C_BANK, JOB_BANK = 0, 4, 5, 6

        identity = sb("identity", [P, P])
        pick = sb("pick", [3 * 2 * N, 2 * N], BF16)
        conv_taps = sb("conv_taps", [P, G, 3])
        negA = sb("negA", [P, N, G])
        halfA = sb("halfA", [P, N, G])
        kappa = sb("kappa", [P, N, G])
        inv_kappa = sb("inv_kappa", [P, N, G])
        coef = sb("coef", [P, N, G])
        delta_lo = sb("delta_lo", [P, G])
        tau_bias = sb("tau_bias", [P, G])
        consts = sb("consts", [P, 3])
        halo = sb("halo", [P, G, 2 * NBLK])
        keep_lim = sb("keep_lim", [P, 2, NBLK])
        low = sb("low", [P, E, E])
        b1_sb = sb("b1_sb", [P, EX * HT])
        b2_sb = sb("b2_sb", [EX, D])
        gw_sb = sb("gw_sb", [P, G, E])
        rs_sb = sb("rs_sb", [P, 1])
        win_sb = sb("win_sb", [P, G, 2 * D])
        wdt_sb = sb("wdt_sb", [P, G, D])
        wbc_sb = sb("wbc_sb", [P, G, 2 * N])
        wout_sb = sb("wout_sb", [P, G, D])
        w1_e = sb("w1_e", [P, 2, G, HID])
        w2_e = sb("w2_e", [P, 2, HT, D])
        nrd = sb("nrd", [P, G, T])
        inv = sb("inv", [P, 2, G, T])
        th = sb("th", [P, 2, G, T])
        abar = sb("abar", [P, 2, G, T])
        hs = sb("hs", [P, G, T])
        carry = sb("carry", [P, N, G])
        u = sb("u", [P, G, T])
        delta = sb("delta", [P, G, T])
        BC3 = sb("BC3", [3 * 2 * N, T], BF16)
        u_next = sb("u_next", [P, G, T])
        delta_next = sb("delta_next", [P, G, T])
        BC3_next = sb("BC3_next", [3 * 2 * N, T], BF16)
        valp = sb("valp", [P, G, T + 2])
        modA = sb("modA", [P, 5, G])
        stats = sb("stats", [P, TPB, 6])
        momA = sb("momA", [P, TPB, 2])
        spreadA = sb("spreadA", [P, TPB])
        norms = sb("norms", [P, NBLK, TPB, 2])
        ys = sb("ys", [P, G, T])
        x1 = sb("x1", [P, TPB, D])
        xn = sb("xn", [P, TPB, D])
        hf = sb("hf", [P, G, T])
        hid = sb("hid", [P, 2, HT, T])
        rows = sb("rows", [P, 2, D])
        modF = sb("modF", [P, 5, G])
        statsF = sb("statsF", [P, TPB, 6])
        momF = sb("momF", [P, TPB, 2])
        spreadF = sb("spreadF", [P, TPB])
        rstdF = sb("rstdF", [P, TPB])
        sco = sb("sco", [P, TPB, E])
        rank = sb("rank", [P, TPB, E])
        gates = sb("gates", [P, TPB, EX])
        gsum = sb("gsum", [P, TPB])

        def flat(ap):
            return ap.rearrange("p a b -> p (a b)")

        xa = flat(u_next[:]).rearrange("p (t d) -> p t d", t=TPB)
        hT = delta_next
        e_neg = ys
        lnw = flat(valp[:])[:, 0:G * T].rearrange("p (g t) -> p g t", g=G)
        gate = hid[:].rearrange("p s h t -> p (s h) t")
        gT = rows[:, 0, :]
        og = xn
        nrd_next = ys
        ysf = flat(ys[:])
        split = ysf[0:2 * N, 0:2 * T].rearrange("p (s t) -> p s t", s=2)
        mid16 = ysf[0:2 * N, 2 * T:2 * T + T // 2].bitcast(BF16)
        xnf = flat(xn[:])
        above = xnf[:, 0:TPB * E * E].rearrange("p (t e f) -> p t e f", t=TPB, e=E)
        ties = xnf[:, TPB * E * E:2 * TPB * E * E].rearrange("p (t e f) -> p t e f", t=TPB, e=E)

        wmod_h = [inv[:].rearrange("p s g t -> p (s g t)"), th[:].rearrange("p s g t -> p (s g t)"),
                  abar[:].rearrange("p s g t -> p (s g t)")]
        wdT = flat(u[:]).rearrange("p (k n) -> p k n", k=G)
        wtau = flat(delta[:]).rearrange("p (k n) -> p k n", k=G)
        small = flat(nrd[:])
        cs = small[:, 0:16].rearrange("p (k b) -> p k b", k=G)
        csilu = small[:, 16:32].rearrange("p (k b) -> p k b", k=G)
        base = small[:, 32:36]
        absA = small[:, 64:64 + N * G].rearrange("p (n g) -> p n g", n=N)
        alog = small[:, 128:128 + N * G].rearrange("p (g n) -> p g n", n=N)
        modh = small[:, 256:256 + 2 * G * NB].rearrange("p (m g b) -> p m g b", m=2, g=G)
        hh = small[:, 512:512 + G * 2 * NBLK].rearrange("p (g i) -> p g i", g=G)
        mrow = flat(x1[:])
        mrow2 = flat(xn[:])
        modrow = [mrow[:, m * D:(m + 1) * D] for m in range(4)] + [mrow2[:, m * D:(m + 1) * D] for m in range(2)]
        signs = flat(hf[:])[:, 0:2 * D].rearrange("p (m d) -> p m d", m=2)
        mags = flat(hf[:])[:, 2 * D:4 * D].rearrange("p (m d) -> p m d", m=2)
        hx = flat(hs[:])[:, 0:D]
        NH = 2 * NBLK

        ld_c, ld_w, ld_m = sem("c_and_A_loaded"), sem("delta_weights_loaded"), [sem(f"wmod_{r}_loaded") for r in range(3)]
        ld, ld_pads, ld_mod = sem("setup_loads"), sem("halo_tokens_loaded"), sem("halo_rows_loaded")
        silu_done, a_done, mod_mm, wdt_mm, setup_v, rows_v, wdt_ev, st_rows = (
            sem("silu_done"), sem("a_done"), sem("mod_mm"), sem("wdt_mm"), sem("setup_vector"), sem("rows_done"),
            sem("wdt_evicted"), sem("rows_stored"))
        base_mm = sem("base_mm")
        row_bank = (4, 5, 6, 0, 1, 2)
        halo_v, halo_sq, halo_mm = sem("halo_steps"), sem("halo_sqrt"), sem("halo_products")
        LOADS = 12
        with nc.Block() as block:
            @block.sync
            def _(sp):
                kp = "(k p) n -> p k n"
                sp.dma_start(cs, cT.rearrange(kp, p=P)).then_inc(ld_c, 16)
                sp.dma_start(alog, A_log.rearrange("(g p) n -> p g n", p=P)).then_inc(ld_c, 16)
                sp.dma_start(wdT, W_deltaT.rearrange(kp, p=P)).then_inc(ld_w, 16)
                sp.dma_start(wtau, W_tau.rearrange(kp, p=P)).then_inc(ld_w, 16)
                sp.dma_start(base, delta_base.rearrange("(k p) -> p k", p=P)).then_inc(ld_w, 16)
                for r in range(3):
                    sp.dma_start(wmod_h[r].rearrange("p (k n) -> p k n", k=G),
                                 wmod[:, 2 * r * D:2 * (r + 1) * D].rearrange(kp, p=P)).then_inc(ld_m[r], 16)
                sp.dma_start(conv_taps[:], conv_w.rearrange("(g p) n -> p g n", p=P)).then_inc(ld, 16)
                sp.dma_start(identity[:], ident).then_inc(ld, 16)
                sp.dma_start(pick[:], onehot).then_inc(ld, 16)
                sp.dma_start(flat(keep_lim[:]), keep.partition_broadcast(P)).then_inc(ld, 16)
                sp.dma_start(flat(low[:]), earlier.partition_broadcast(P)).then_inc(ld, 16)
                sp.dma_start(b1_sb[:], b1.rearrange("(k p) -> p k", p=P)).then_inc(ld, 16)
                sp.dma_start(b2_sb[:], b2).then_inc(ld, 16)
                sp.dma_start(gw_sb[:], gate_W.rearrange(kp, p=P)).then_inc(ld, 16)
                sp.dma_start(rs_sb[:], route_scale.partition_broadcast(P)).then_inc(ld, 16)
                sp.dma_start(win_sb[:], W_in.rearrange(kp, p=P)).then_inc(ld, 16)
                sp.dma_start(wbc_sb[:], W_BC.rearrange(kp, p=P)).then_inc(ld, 16)
                sp.dma_start(wout_sb[:], W_out.rearrange(kp, p=P)).then_inc(ld, 16)
                xt = x_flat.rearrange("(i t) d -> i t d", t=T)
                sp.dma_start(hx[0:1, :], x_flat[0:1, :]).then_inc(ld_pads, 16)
                sp.dma_start(hx[1:NBLK, :], xt[0:NBLK - 1, T - 1, :]).then_inc(ld_pads, 16)
                sp.dma_start(hx[NBLK:NH - 1, :], xt[1:NBLK, 0, :]).then_inc(ld_pads, 16)
                sp.dma_start(hx[NH - 1:NH, :], x_flat[0:1, :]).then_inc(ld_pads, 16)
                sp.wait_ge(rows_v, 2)
                hr = h_rows.rearrange("(b r) (m d) -> r b m d", r=PER, m=MODS)
                for r in range(PER):
                    sp.dma_start(hr[r, :, 0:4, :], mrow[0:NB, :].rearrange("b (m d) -> b m d", m=4)).then_inc(st_rows, 16)
                    sp.dma_start(hr[r, :, 4:6, :], mrow2[0:NB, 0:2 * D].rearrange("b (m d) -> b m d", m=2)).then_inc(st_rows, 16)
                sp.wait_ge(st_rows, 32 * PER)
                hb = h_rows.rearrange("(b r) (m g p) -> r m g p b", r=PER, m=MODS, p=P)
                for m in range(2):
                    for g in range(G):
                        sp.dma_start(modh[:, m, g, :], hb[0, m, g]).then_inc(ld_mod, 16)
                sp.wait_ge(ld_mod, 32 * G)

            @block.scalar
            def _(act):
                act.wait_ge(ld_c, 32)
                nc.scalar.activation(csilu, cs, ACT.Silu).then_inc(silu_done, 1)
                for g in range(G):
                    ins = nc.scalar.activation(absA[:, :, g], alog[:, g, :], ACT.Exp)
                ins.then_inc(a_done, 1)
                act.wait_ge(wdt_mm, 1)
                for i in range(G):
                    nc.scalar.activation(wdt_sb[:, i, :], ps[:, i, :], ACT.Identity).then_inc(wdt_ev, 1)
                act.wait_ge(halo_v, 2)
                nc.scalar.activation(spreadA[0:NH, 0:1], momA[0:NH, 0, 1:2], ACT.Sqrt, bias=consts[0:NH, 1:2]).then_inc(halo_sq, 1)

            @block.tensor
            def _(pe):
                pe.wait_ge(ld_w, 48)
                for i in range(G):
                    for k in range(G):
                        mm = nc.tensor.matmul(ps[:, i, :], wdT[:, k, i * P:(i + 1) * P], wtau[:, k, :],
                                              start=(k == 0), stop=(k == G - 1))
                mm.then_inc(wdt_mm, 1)
                for g in range(G):
                    for k in range(G):
                        mm = nc.tensor.matmul(ps[:, 7, g:g + 1], wtau[:, k, g * P:(g + 1) * P], base[:, k:k + 1],
                                              start=(k == 0), stop=(k == G - 1))
                mm.then_inc(base_mm, 1)
                pe.wait_ge(silu_done, 1)
                for m in range(MODS):
                    if m % 2 == 0:
                        pe.wait_ge(ld_m[m // 2], 16)
                    if m == 3:
                        pe.wait_ge(wdt_ev, G)
                    w = wmod_h[m // 2].rearrange("p (k n) -> p k n", k=G)
                    for k in range(G):
                        mm = nc.tensor.matmul(ps[0:NB, row_bank[m], :], csilu[:, k, :], w[:, k, (m % 2) * D:(m % 2 + 1) * D],
                                              start=(k == 0), stop=(k == G - 1))
                mm.then_inc(mod_mm, 1)
                pe.wait_ge(ld, 16 * LOADS)
                pe.wait_ge(halo_v, 4)
                for g in range(G):
                    mm = nc.tensor.transpose(ps[:, 5, g * NH:(g + 1) * NH], hx[0:NH, g * P:(g + 1) * P], identity[0:NH, 0:NH])
                mm.then_inc(halo_mm, 1)
                pe.wait_ge(halo_v, 4 + 4 * G)
                for m in range(G):
                    for k in range(G):
                        mm = nc.tensor.matmul(ps[:, 6, m * NH:(m + 1) * NH], win_sb[:, k, m * P:(m + 1) * P], hh[:, k, :],
                                              start=(k == 0), stop=(k == G - 1))
                mm.then_inc(halo_mm, 1)

            @block.vector
            def _(dve):
                v = nc.vector
                count = [0]

                def done(ins):
                    count[0] += 1
                    ins.then_inc(setup_v, 1)

                dve.wait_ge(mod_mm, 1)
                for m, add in enumerate((0.0, 1.0, 0.0, 0.0, 1.0, 0.0)):
                    done(v.tensor_scalar(modrow[m][0:NB], ps[0:NB, row_bank[m], :], add, None, ALU.add))
                dve.wait_ge(setup_v, 6)
                for i, m in enumerate((R_GA, R_GB)):
                    done(v.tensor_scalar(signs[0:NB, i, :], modrow[m][0:NB], 0.0, 2.0, ALU.is_ge, ALU.mult))
                    done(v.scalar_tensor_tensor(mags[0:NB, i, :], modrow[m][0:NB], -1.0, modrow[m][0:NB], ALU.mult, ALU.max))
                dve.wait_ge(setup_v, 10)
                for i in range(2):
                    done(v.tensor_scalar(signs[0:NB, i, :], signs[0:NB, i, :], -1.0, None, ALU.add))
                    done(v.tensor_scalar(mags[0:NB, i, :], mags[0:NB, i, :], 0.25, None, ALU.max))
                dve.wait_ge(setup_v, 14)
                v.tensor_tensor(modrow[R_GB][0:NB], signs[0:NB, 1, :], mags[0:NB, 1, :], ALU.mult).then_inc(rows_v, 1)
                v.tensor_tensor(modrow[R_GA][0:NB], signs[0:NB, 0, :], mags[0:NB, 0, :], ALU.mult).then_inc(rows_v, 1)
                dve.wait_ge(base_mm, 1)
                done(v.tensor_copy(tau_bias[:], ps[:, 7, 0:G]))
                dve.wait_ge(a_done, 1)
                done(v.tensor_scalar(negA[:], absA, -1.0, None, ALU.mult))
                done(v.tensor_scalar(halfA[:], absA, -0.5, None, ALU.mult))
                done(v.tensor_scalar(inv_kappa[:], absA, 1.0 / DA_EPS, None, ALU.mult))
                done(v.memset(consts[:, 0:1], 1.0))
                done(v.memset(consts[:, 1:2], LN_EPS))
                done(v.memset(consts[:, 2:3], 1e-18))
                done(v.memset(carry[:], 0.0))
                dve.wait_ge(setup_v, count[0])
                done(v.reciprocal(kappa[:], inv_kappa[:]))
                done(v.reciprocal(coef[:], negA[:]))
                dve.wait_ge(setup_v, count[0])
                done(v.tensor_tensor(coef[:], coef[:], kappa[:], ALU.mult))
                done(v.tensor_reduce(delta_lo[:], kappa[:].rearrange("p n g -> p g n"), AX_X, ALU.max))
                dve.wait_ge(setup_v, count[0])
                done(v.tensor_scalar(delta_lo[:], delta_lo[:], 1.0 / Y_CAP, None, ALU.mult))
                dve.wait_ge(ld_pads, 64)
                v.bn_stats(stats[0:NH, 0, :], hx[0:NH, :]).then_inc(halo_v, 1)
                dve.wait_ge(halo_v, 1)
                v.bn_aggr(momA[0:NH, 0, :], stats[0:NH, 0, :]).then_inc(halo_v, 1)
                dve.wait_ge(halo_sq, 1)
                v.reciprocal(spreadA[0:NH, 1:2], spreadA[0:NH, 0:1]).then_inc(halo_v, 1)
                dve.wait_ge(halo_v, 3)
                v.tensor_scalar(hx[0:NH, :], hx[0:NH, :], momA[0:NH, 0, 0:1], spreadA[0:NH, 1:2], ALU.subtract,
                                ALU.mult).then_inc(halo_v, 1)
                dve.wait_ge(ld_mod, 32 * G)
                dve.wait_ge(halo_mm, 1)
                n = 4
                for step_, (m, op) in enumerate(((1, ALU.mult), (0, ALU.add))):
                    if step_:
                        dve.wait_ge(halo_v, n)
                    for g in range(G):
                        for side in range(2):
                            dst = hh[:, g, side * NBLK:(side + 1) * NBLK].rearrange("p (b r) -> p b r", r=PER)
                            src = ps[:, 5, g * NH + side * NBLK:g * NH + (side + 1) * NBLK].rearrange("p (b r) -> p b r", r=PER)
                            v.tensor_tensor(dst, dst if step_ else src,
                                            modh[:, m, g, :].unsqueeze(2).broadcast_to([P, NB, PER]), op).then_inc(halo_v, 1)
                            n += 1
                dve.wait_ge(halo_mm, 2)
                v.tensor_copy(flat(halo[:]), ps[:, 6, 0:G * NH]).then_inc(halo_v, 1)
                dve.wait_ge(halo_v, n + 1)
                v.memset(halo[:, :, 0:NBLK:PER], 0.0)
                v.memset(halo[:, :, NBLK + PER - 1:NH:PER], 0.0).then_inc(halo_v, 1)
                dve.wait_ge(halo_v, n + 2)
                dve.wait_ge(setup_v, count[0])

        inv_steps, exp_done, ratio_done, em1_done, factor_done = (
            sem("inv_steps"), sem("exp_done"), sem("ratio_done"), sem("em1_done"), sem("factor_done"))
        w_done, bu_done, scan_done, carry_done, hC_done = (
            sem("uB_done"), sem("bu_done"), sem("scan_done"), sem("carry_done"), sem("hC_done"))
        B_ready, C_ready, y_summed, y_taken = sem("B_ready"), sem("C_ready"), sem("y_summed"), sem("y_taken")
        delta_moved, u_moved, bc_moved, nrd_moved = sem("delta_moved"), sem("u_moved"), sem("bc_moved"), sem("nrd_moved")
        a_ld, a_stat, a_sqrt, a_rstd, a_xn, a_job, a_aev, a_edge, a_v, a_conv, a_silu = (
            sem("a_loaded"), sem("a_stats"), sem("a_sqrt"), sem("a_rstd"), sem("a_normalized"), sem("a_jobs"),
            sem("a_evicted"), sem("a_edges"), sem("a_conv_steps"), sem("a_conv"), sem("a_silu"))
        a_e, a_corr, a_ln, a_diff, a_delta, a_bc, a_floor, a_rd, a_newton, a_norm = (
            sem("a_exp_steps"), sem("a_correction_steps"), sem("a_ln"), sem("a_log1p"), sem("a_delta"), sem("a_bc_steps"),
            sem("a_delta_floored"), sem("a_reciprocal_steps"), sem("a_newton_steps"), sem("a_norm"))
        f_ld, f_xn, f_job, f_aev, f_dev, f_gated, f_res, f_stat, f_sqrt, f_rstd, f_xn2 = (
            sem("f_loaded"), sem("f_normalized"), sem("f_jobs"), sem("f_evicted_act"),
            sem("f_evicted_dve"), sem("f_gated"), sem("f_resid_steps"), sem("f_stats"), sem("f_sqrt"), sem("f_rstd"),
            sem("f_normalized2"))
        f_top, f_gates, f_wl, f_fin, f_out, f_st = (
            sem("f_top_steps"), sem("f_gates"), [sem("expert_loaded_0"), sem("expert_loaded_1")], sem("f_final"),
            sem("f_out_done"), sem("f_stored"))

        JA_T, JA_VAL, JA_P, JA_BC, JA = 0, G, 2 * G, 3 * G, 3 * G + 1
        JF_T, JF_GATE, JF_OUT, JF_T2, JF_LOG, JF_W1_0 = 0, G, 2 * G, 2 * G + TPB, 3 * G + TPB, 3 * G + TPB + 1
        JF = 3 * G + TPB + 1 + 1 + EX * (HT + TPB)
        AEV_F = 3 * G + 1 + EX * HT
        DEV_F = TPB + 1 + EX * TPB

        def aev_gelu(e):
            return 3 * G + 1 + e * HT

        def dev_w2(e):
            return TPB + e * TPB + (e > 0)

        DEV_GT = 2 * TPB

        def f_job_no(what, e=0):
            order = [("t", 0)] * G + [("gate", 0)] * G + [("out", 0)] * TPB + [("t2", 0)] * G + [("log", 0)]
            order += [("w1", 0)] * HT
            for i in range(E):
                order += [("w2", i)] * TPB + [("w1", i + 1)] * HT
                if i == 0:
                    order += [("gT", 0)]
            order += [("w2", E)] * TPB
            assert len(order) == JF
            return order.index((what, e))

        SLOT_W2 = N - EX

        def sync_block(sp, it, scan, A, F):
            a, f = it + 1, it - 1
            kp = "(k p) n -> p k n"

            def load_w1(e):
                sp.dma_start(w1_e[:, e % 2], W1[:, e * HID:(e + 1) * HID].rearrange(kp, p=P)).then_inc(f_wl[e % 2], 16)

            def load_w2(e):
                sp.dma_start(w2_e[:, e % 2], W2[e * HID:(e + 1) * HID, :].rearrange(kp, p=P)).then_inc(f_wl[e % 2], 16)

            if F:
                sp.wait_ge(f_out, f + 1)
                block_f = f * T if isinstance(f, int) else sp.snap(f * T)
                row = h_rows[bass.ds(f, 1), :]
                sp.dma_start(x1[:], x_flat[bass.ds(block_f, T), :].rearrange("(t p) d -> p t d", p=P)).then_inc(f_ld, 16)
                sp.dma_start(modF[:], row[:, 0:5 * D].rearrange("o (m g p) -> p (o m) g", m=5, p=P)).then_inc(f_ld, 16)
                for i, m in enumerate((R_GA, R_GB)):
                    sp.dma_start(rows[:, i, :], row[:, m * D:(m + 1) * D].partition_broadcast(P)
                                 .rearrange("p o d -> p (o d)")).then_inc(f_ld, 16)
                load_w1(0)
                load_w2(0)
            if A:
                ge(sp, u_moved, it + 1)
                ge(sp, w_done, it * N + 1 if scan else 0)
                ge(sp, a_aev, (a - 1) * (3 * G) + G)
            if F:
                load_w1(1)
            if A:
                sp.dma_start(xa, x_flat[bass.ds(a * T, T), :].rearrange("(t p) d -> p t d", p=P)).then_inc(a_ld, 16)
                sp.dma_start(modA[:], h_rows[bass.ds(a, 1), 0:5 * D].rearrange("o (m g p) -> p (o m) g", m=5, p=P)).then_inc(a_ld, 16)
            if F:
                load_w2(1)
                for e in range(2, EX):
                    sp.wait_ge(f_job, f * JF + f_job_no("w2", e - 2) + TPB)
                    load_w1(e)
                    load_w2(e)
                sp.wait_ge(f_out, f + 2)
                sp.dma_start(out_flat[bass.ds(block_f, T), :].rearrange("(t p) d -> p t d", p=P), xn[:]).then_inc(f_st, 16)

        def act_block(act, it, scan, A, F, prev):
            s = nc.scalar
            a, f = it + 1, it - 1

            def evict(kind, dst, bank, func, **kw):
                s.activation(dst, ps[:, bank, :], func, **kw).then_inc(a_aev if kind == "A" else f_aev, 1)

            def normalize(src, dst, i, done):
                for tt in range(TPB):
                    nm = norms[:, bass.ds(i, 1), tt, :].rearrange("p o s -> p (o s)")
                    ins = s.activation(dst[:, tt, :], src[:, tt, :], ACT.Identity, bias=nm[:, 0:1], scale=nm[:, 1:2])
                ins.then_inc(done, 1)

            def take_p(groups):
                for g in groups:
                    act.wait_ge(a_job, a * JA + JA_P + g + 1)
                    evict("A", delta_next[:, g, :], bank_A[JA_P + g], ACT.Identity, bias=tau_bias[:, g:g + 1])

            def chain(n, between=None):
                c = it * N + n
                nn = n % N
                p = nn % 2
                d, nr = (delta_next, nrd_next) if n == N else (delta, nrd)
                if n == N:
                    ge(act, a_newton, (it + 2) * 2)
                elif n == 1:
                    ge(act, nrd_moved, it + 1)
                ge(act, scan_done, c - 1)
                for g in range(G):
                    ins = s.activation(inv[:, p, g, :], nr[:, g, :], ACT.Square, bias=consts[:, 0:1], scale=kappa[:, nn, g:g + 1])
                ins.then_inc(inv_steps, 1)
                ge(act, inv_steps, 3 * c + 1)
                s.activation(inv[:, p], inv[:, p], ACT.Ln, bias=consts[:, 2:3]).then_inc(inv_steps, 1)
                ge(act, inv_steps, 3 * c + 2)
                s.activation(inv[:, p], inv[:, p], ACT.Exp, scale=-1.0).then_inc(inv_steps, 1)
                if between is not None:
                    between()
                if n == N:
                    ge(act, a_delta, it + 2)
                elif n == 1:
                    ge(act, delta_moved, it + 1)
                for g in range(G):
                    s.activation(th[:, p, g, :], d[:, g, :], ACT.Tanh, scale=halfA[:, nn, g:g + 1])
                for g in range(G):
                    ins = s.activation(abar[:, p, g, :], d[:, g, :], ACT.Exp, scale=negA[:, nn, g:g + 1])
                ins.then_inc(exp_done, 1)

            for slot in range(N):
                if scan and slot + 1 < N:
                    chain(slot + 1, (lambda: take_p(range(2))) if A and slot == 6 else None)
                elif A and slot + 1 == N:
                    chain(N)
                    ge(act, ratio_done, it * N + N)
                    s.activation(nrd[:], nrd_next[:], ACT.Identity).then_inc(nrd_moved, 1)
                    s.activation(delta[:], delta_next[:], ACT.Identity).then_inc(delta_moved, 1)
                    ge(act, w_done, it * N + N)
                    act.wait_ge(a_silu, a + 1)
                    s.activation(u[:], u_next[:], ACT.Identity).then_inc(u_moved, 1)
                if prev and slot == 0:
                    ge(act, y_summed, it * N)
                    ge(act, nrd_moved, it + 1 if scan else it)
                    s.activation(ys[:], ps[:, Y_BANK:Y_BANK + G, :], ACT.Identity).then_inc(y_taken, 1)
                if F and slot == 0:
                    act.wait_ge(f_ld, f * 64 + 64)
                    for g in range(G):
                        act.wait_ge(f_job, f * JF + JF_T + g + 1)
                        evict("F", hf[:, g, :], bank_F[JF_T + g], ACT.Identity, bias=modF[:, 0, g:g + 1], scale=modF[:, 1, g:g + 1])
                if A and slot == 1:
                    ge(act, a_stat, a * (TPB + 1) + TPB + 1)
                    s.activation(spreadA[:], momA[:, :, 1], ACT.Sqrt, bias=consts[:, 1:2]).then_inc(a_sqrt, 1)
                if F and slot == 1:
                    for g in range(G):
                        act.wait_ge(f_job, f * JF + JF_GATE + g + 1)
                        evict("F", gate[:, g, :], bank_F[JF_GATE + g], ACT.Silu)
                if A and slot == 2:
                    act.wait_ge(a_norm, a + 1)
                    normalize(xa, xa, a, a_xn)
                if A and slot == 3:
                    ge(act, a_ld, a * 32 + 32)
                    for g in range(G):
                        act.wait_ge(a_job, a * JA + JA_T + g + 1)
                        evict("A", hT[:, g, :], bank_A[JA_T + g], ACT.Identity, bias=modA[:, 0, g:g + 1], scale=modA[:, 1, g:g + 1])
                if F and slot == 3:
                    act.wait_ge(f_stat, f * (TPB + 1) + TPB + 1)
                    s.activation(spreadF[:], momF[:, :, 1], ACT.Sqrt, bias=consts[:, 1:2]).then_inc(f_sqrt, 1)
                if A and slot in (3, 4):
                    if slot == 3:
                        ge(act, a_newton, a * 2)
                    for g in (range(2) if slot == 3 else range(2, G)):
                        act.wait_ge(a_job, a * JA + JA_VAL + g + 1)
                        s.activation(u_next[:, g, :], ps[:, bank_A[JA_VAL + g], :], ACT.Identity,
                                     scale=conv_taps[:, g, 1:2])
                        evict("A", valp[:, g, 1:T + 1], bank_A[JA_VAL + g], ACT.Identity)
                if F and slot == 4:
                    for g in range(G):
                        act.wait_ge(f_job, f * JF + JF_T2 + g + 1)
                        evict("F", hf[:, g, :], bank_F[JF_T2 + g], ACT.Identity, bias=modF[:, 3, g:g + 1], scale=modF[:, 4, g:g + 1])
                if A and slot == 5:
                    act.wait_ge(a_conv, a + 1)
                    s.activation(u_next[:], u_next[:], ACT.Silu).then_inc(a_silu, 1)
                if F and slot == 5:
                    act.wait_ge(f_job, f * JF + JF_LOG + 1)
                    s.activation(flat(sco[:]), ps[:, bank_F[JF_LOG], 0:TPB * E], ACT.Sigmoid).then_inc(f_aev, 1)
                if A and slot == 6:
                    take_p(range(2 if scan else 0, G))
                    act.wait_ge(a_aev, a * (3 * G) + 3 * G)
                    if F:
                        act.wait_ge(f_job, f * JF + JF_OUT + TPB)
                    s.activation(e_neg[:], delta_next[:], ACT.Abs).then_inc(a_e, 1)
                    act.wait_ge(a_e, a * 2 + 1)
                    s.activation(e_neg[:], e_neg[:], ACT.Exp, scale=-1.0).then_inc(a_e, 1)
                if A and slot == 9:
                    act.wait_ge(a_corr, a * 2 + 2)
                    s.activation(lnw, lnw, ACT.Ln).then_inc(a_ln, 1)
                if A and slot == 12:
                    act.wait_ge(a_floor, a + 1)
                    act.wait_ge(a_bc, a * 6 + 6)
                    s.activation(nrd_next[:], lnw, ACT.Ln).then_inc(a_rd, 1)
                    act.wait_ge(a_rd, a * 2 + 1)
                    s.activation(nrd_next[:], nrd_next[:], ACT.Exp, scale=-1.0).then_inc(a_rd, 1)
                if F and (slot == 5 or SLOT_W2 <= slot < N - 1):
                    e = 0 if slot == 5 else slot - SLOT_W2 + 1
                    if e >= 2:
                        act.wait_ge(f_job, f * JF + f_job_no("w2", e - 2) + TPB)
                    elif e == 0:
                        act.wait_ge(f_gated, f + 1)
                    for h in range(HT):
                        act.wait_ge(f_job, f * JF + f_job_no("w1", e) + h + 1)
                        evict("F", hid[:, e % 2, h, :], bank_F[f_job_no("w1", e) + h], ACT.Gelu,
                              bias=b1_sb[:, e * HT + h:e * HT + h + 1])

        def pe_slots(A, F):
            early = {s_: [] for s_ in range(N)}
            late = {s_: [] for s_ in range(N)}
            if F:
                late[0] += [("F", "t", 0, g) for g in range(G)]
                early[1] += [("F", "gate", 0, g) for g in range(G)]
                early[2] += [("F", "out", 0, t_) for t_ in range(TPB)]
            if A:
                early[3] += [("A", "t", 0, g) for g in range(G)]
                late[3] += [("A", "val", 0, g) for g in range(2)]
                early[4] += [("A", "val", 0, g) for g in range(2, G)]
            if F:
                early[4] += [("F", "t2", 0, g) for g in range(G)]
            if F:
                early[5] += [("F", "log", 0, 0)] + [("F", "w1", 0, h) for h in range(HT)]
            if A:
                late[5] += [("A", "p", 0, g) for g in range(2)]
                early[6] += [("A", "p", 0, g) for g in range(2, G)]
            if F:
                for e in range(EX):
                    early[SLOT_W2 + e] += [("F", "w2", e, t_) for t_ in range(TPB)]
                    if e + 1 < EX:
                        early[SLOT_W2 + e] += [("F", "w1", e + 1, h) for h in range(HT)]
                late[SLOT_W2] += [("F", "gT", 0, 0)]
            if A:
                late[10] += [("A", "bc", 0, 0)]
            return early, late

        def plan_banks(A, F):
            early, late = pe_slots(A, F)
            plan, last, n, nA, nF = {}, {}, 0, 0, 0
            for s_ in range(N):
                for job in early[s_] + late[s_]:
                    bank = JOB_BANK + n % 2
                    no = nA if job[0] == "A" else nF
                    plan[(job[0], no)] = (bank, last.get(bank))
                    last[bank] = (job, no)
                    n += 1
                    nA += job[0] == "A"
                    nF += job[0] == "F"
            return plan, last

        def evicted(job, no, a, f):
            kind, what, e, i = job
            if kind == "A":
                return (a_bc, a * 6 + 2) if what == "bc" else (a_aev, a * (3 * G) + no + 1)
            if what in ("out", "gT", "w2"):
                return f_dev, f * DEV_F + 1 + {"out": i, "gT": DEV_GT, "w2": dev_w2(e) + i}[what] + 1
            return f_aev, f * AEV_F + {"t": i, "gate": G + i, "t2": 2 * G + i, "log": 3 * G, "w1": aev_gelu(e) + i}[what] + 1

        def pe_block(pe, it, scan, A, F, prev, plan):
            t = nc.tensor
            a, f = it + 1, it - 1
            early, late = pe_slots(A, F)
            numbers = {"A": 0, "F": 0}

            def job(kind, what, e, i):
                no = numbers[kind]
                numbers[kind] += 1
                bank, before = plan[(kind, no)]
                if before is not None:
                    sm, val = evicted(before[0], before[1], a, f)
                    ge(pe, sm, val)
                elif F:
                    pe.wait_ge(f_dev, f * DEV_F + 1)
                o = ps[:, bank, :]
                if what == "t":
                    src = xa if kind == "A" else xn
                    if i == 0:
                        pe.wait_ge(a_xn if kind == "A" else f_xn, (a if kind == "A" else f) + 1)
                    for tt in range(TPB):
                        mm = t.transpose(o[:, tt * P:(tt + 1) * P], src[:, tt, i * P:(i + 1) * P], identity[:])
                elif what == "val" or what == "gate":
                    if i == 0:
                        pe.wait_ge(a_aev if kind == "A" else f_aev, (a * (3 * G) if kind == "A" else f * AEV_F) + G)
                    m = i + (G if what == "gate" else 0)
                    h = hT if kind == "A" else hf
                    for k in range(G):
                        mm = t.matmul(o, win_sb[:, k, m * P:(m + 1) * P], h[:, k, :], start=(k == 0), stop=(k == G - 1))
                elif what == "p":
                    if i == 0:
                        pe.wait_ge(a_silu, a + 1)
                    for k in range(G):
                        mm = t.matmul(o, wdt_sb[:, k, i * P:(i + 1) * P], u_next[:, k, :], start=(k == 0), stop=(k == G - 1))
                elif what == "bc":
                    for k in range(G):
                        mm = t.matmul(o[0:2 * N, :], wbc_sb[:, k, :], u_next[:, k, :], start=(k == 0), stop=(k == G - 1))
                elif what == "out":
                    if i == 0:
                        pe.wait_ge(f_gated, f + 1)
                    for k in range(G):
                        t.matmul(o, ys[:, k, i * P:(i + 1) * P], wout_sb[:, k, :], start=(k == 0), stop=False,
                                 skip_group_check=True)
                    for k in range(G):
                        mm = t.matmul(o[:, k * P:(k + 1) * P], hf[:, k, i * P:(i + 1) * P], identity[:], start=False,
                                      stop=(k == G - 1), skip_group_check=True)
                elif what == "t2":
                    if i == 0:
                        pe.wait_ge(f_xn2, f + 1)
                    for tt in range(TPB):
                        mm = t.transpose(o[:, tt * P:(tt + 1) * P], xn[:, tt, i * P:(i + 1) * P], identity[:])
                elif what == "log":
                    pe.wait_ge(f_aev, f * AEV_F + 3 * G)
                    for tt in range(TPB):
                        for k in range(G):
                            mm = t.matmul(o[:, tt * E:(tt + 1) * E], hf[:, k, tt * P:(tt + 1) * P], gw_sb[:, k, :],
                                          start=(k == 0), stop=(k == G - 1))
                elif what == "w1":
                    if i == 0:
                        pe.wait_ge(f_wl[e % 2], f * (32 * ((EX + 1 - e % 2) // 2)) + 32 * (e // 2 + 1))
                    for k in range(G):
                        mm = t.matmul(o, w1_e[:, e % 2, k, i * P:(i + 1) * P], hf[:, k, :], start=(k == 0), stop=(k == G - 1))
                elif what == "gT":
                    pe.wait_ge(f_gates, f + 1)
                    for tt in range(TPB):
                        mm = t.transpose(o[0:EX, tt * P:(tt + 1) * P], gates[:, tt, :], identity[:])
                elif what == "w2":
                    if i == 0:
                        pe.wait_ge(f_aev, f * AEV_F + aev_gelu(e) + HT)
                    if e == E:
                        if i == 0:
                            pe.wait_ge(f_dev, f * DEV_F + 1 + DEV_GT + 1)
                        t.matmul(o, gT[0:EX, i * P:(i + 1) * P], b2_sb[:, :], start=True, stop=False)
                    for h in range(HT):
                        mm = t.matmul(o, hid[:, e % 2, h, i * P:(i + 1) * P], w2_e[:, e % 2, h, :],
                                      start=(h == 0 and e < E), stop=(h == HT - 1))
                mm.then_inc(a_job if kind == "A" else f_job, 1)

            def spread(bank, n, src, ready):
                t.matmul(ps[:, bank, :], pick[:, n:n + 1].broadcast_to([3 * 2 * N, P]), src[:, :], start=True,
                         stop=True).then_inc(ready, 1)

            def sum_y(n, c):
                ge(pe, hC_done, c)
                if n == 0:
                    ge(pe, y_taken, it)
                for g in range(G):
                    mm = t.matmul(ps[:, Y_BANK + g, :], identity[:], hs[:, g, :], start=(n == 0), stop=(n == N - 1),
                                  skip_group_check=True)
                mm.then_inc(y_summed, 1)

            for slot in range(N):
                if slot == 0 and prev:
                    sum_y(N - 1, it * N)
                elif slot and scan:
                    sum_y(slot - 1, it * N + slot)
                if scan:
                    if slot == 0:
                        pe.wait_ge(bc_moved, it + 1)
                        ge(pe, hC_done, it * N)
                    spread(C_BANK, N + slot, BC3, C_ready)
                for j in early[slot]:
                    job(*j)
                if scan and slot + 1 < N:
                    pe.wait_ge(w_done, it * N + slot + 1)
                    spread(B_BANK, slot + 1, BC3, B_ready)
                elif A and slot + 1 == N:
                    ge(pe, w_done, it * N + N)
                    pe.wait_ge(a_bc, a * 6 + 6)
                    spread(B_BANK, 0, BC3_next, B_ready)
                for j in late[slot]:
                    job(*j)

        def dve_block(dve, it, scan, A, F):
            v = nc.vector
            a, f = it + 1, it - 1

            def w2_sum(e, tt):
                dve.wait_ge(f_job, f * JF + f_job_no("w2", e) + tt + 1)
                src = ps[:, bank_F[f_job_no("w2", e) + tt], :]
                if e == 0:
                    dve.wait_ge(f_gates, f + 1)
                    ins = v.tensor_scalar(xn[:, tt, :], src, gates[:, tt, 0:1], None, ALU.mult)
                else:
                    dve.wait_ge(f_dev, f * DEV_F + 1 + dev_w2(e - 1) + tt + 1)
                    ins = v.scalar_tensor_tensor(xn[:, tt, :], src, gates[:, tt, e:e + 1], xn[:, tt, :], ALU.mult, ALU.add)
                ins.then_inc(f_dev, 1)

            def normalize_f1():
                dve.wait_ge(f_ld, f * 64 + 64)
                dve.wait_ge(f_st, f * 16 + 1)
                for tt in range(TPB):
                    nm = norms[:, bass.ds(f, 1), tt, :].rearrange("p o s -> p (o s)")
                    ins = v.tensor_scalar(xn[:, tt, :], x1[:, tt, :], nm[:, 1:2], nm[:, 0:1], ALU.mult, ALU.add)
                ins.then_inc(f_xn, 1)

            def stats_of(src, st, mom, sm, base_):
                for tt in range(TPB):
                    v.bn_stats(st[:, tt, :], src[:, tt, :]).then_inc(sm, 1)
                dve.wait_ge(sm, base_ + TPB)
                v.memset(gates[:, :, E:EX], 1.0)
                for tt in range(TPB):
                    ins = v.bn_aggr(mom[:, tt, :], st[:, tt, :])
                ins.then_inc(sm, 1)

            def stats_A():
                dve.wait_ge(a_ld, a * 32 + 32)
                stats_of(xa, stats, momA, a_stat, a * (TPB + 1))

            def norm_A():
                dve.wait_ge(a_sqrt, a + 1)
                v.reciprocal(spreadA[:], spreadA[:]).then_inc(a_rstd, 1)
                dve.wait_ge(a_rstd, a + 1)
                nm = norms[:, bass.ds(a, 1), :, :].rearrange("p o t s -> p (o t) s")
                v.tensor_copy(nm[:, :, 1], spreadA[:])
                v.scalar_tensor_tensor(nm[:, :, 0], momA[:, :, 0], -1.0, spreadA[:], ALU.mult, ALU.mult).then_inc(a_norm, 1)

            def gated():
                dve.wait_ge(y_taken, it)
                dve.wait_ge(f_aev, f * AEV_F + 2 * G)
                v.tensor_tensor(ys[:], ys[:], gate, ALU.mult).then_inc(f_gated, 1)

            def take_out(tt):
                dve.wait_ge(f_job, f * JF + JF_OUT + tt + 1)
                v.tensor_tensor(og[:, tt, :], ps[:, bank_F[JF_OUT + tt], :], rows[:, 0, :], ALU.mult).then_inc(f_dev, 1)

            def resid_after():
                dve.wait_ge(f_dev, f * DEV_F + 1 + TPB)
                v.tensor_tensor(x1[:], x1[:], og[:], ALU.add).then_inc(f_res, 1)
                dve.wait_ge(f_res, f + 1)
                stats_of(x1, statsF, momF, f_stat, f * (TPB + 1))

            def normalize_f2():
                dve.wait_ge(f_sqrt, f + 1)
                v.reciprocal(rstdF[:], spreadF[:]).then_inc(f_rstd, 1)
                dve.wait_ge(f_rstd, f + 1)
                for tt in range(TPB):
                    ins = v.tensor_scalar(xn[:, tt, :], x1[:, tt, :], momF[:, tt, 0:1], rstdF[:, tt:tt + 1],
                                          ALU.subtract, ALU.mult)
                ins.then_inc(f_xn2, 1)

            def conv():
                dve.wait_ge(a_aev, a * (3 * G) + 2 * G)
                v.tensor_copy(valp[:, :, 0:1], halo[:, :, bass.ds(a, 1)])
                v.tensor_copy(valp[:, :, T + 1:T + 2], halo[:, :, bass.ds(a + NBLK, 1)]).then_inc(a_edge, 1)
                dve.wait_ge(a_edge, a + 1)
                for tap in (0, 2):
                    if tap == 2:
                        dve.wait_ge(a_v, a + 1)
                    for g in range(G):
                        ins = v.scalar_tensor_tensor(u_next[:, g, :], valp[:, g, tap:T + tap], conv_taps[:, g, tap:tap + 1],
                                                     u_next[:, g, :], ALU.mult, ALU.add)
                    ins.then_inc(a_v if tap == 0 else a_conv, 1)

            def top_two():
                n = [0]

                def step(ins):
                    n[0] += 1
                    ins.then_inc(f_top, 1)
                    dve.wait_ge(f_top, f * 8 + n[0])

                dve.wait_ge(f_aev, f * AEV_F + 3 * G + 1)
                step(v.tensor_scalar(sco[:], sco[:], rs_sb[:, 0:1], None, ALU.mult))
                other = sco[:].unsqueeze(2).broadcast_to([P, TPB, E, E])
                mine = sco[:].unsqueeze(3).broadcast_to([P, TPB, E, E])
                v.tensor_tensor(above, other, mine, ALU.is_gt)
                step(v.tensor_tensor(ties, other, mine, ALU.is_equal))
                step(v.tensor_tensor(ties, ties, low[:].unsqueeze(1).broadcast_to([P, TPB, E, E]), ALU.mult))
                step(v.tensor_tensor(above, above, ties, ALU.add))
                step(v.tensor_reduce(rank[:], above, AX_X, ALU.add))
                step(v.scalar_tensor_tensor(gates[:, :, 0:E], rank[:], 1.5, sco[:], ALU.is_lt, ALU.mult))
                step(v.tensor_reduce(gsum[:], gates[:, :, 0:E], AX_X, ALU.add))
                step(v.reciprocal(gsum[:], gsum[:]))
                assert n[0] == 8
                v.tensor_tensor(gates[:, :, 0:E], gates[:, :, 0:E], gsum[:].unsqueeze(2).broadcast_to([P, TPB, E]),
                                ALU.mult).then_inc(f_gates, 1)

            def take_gT():
                no = f_job_no("gT")
                dve.wait_ge(f_job, f * JF + no + 1)
                v.tensor_copy(gT[0:EX, :], ps[0:EX, bank_F[no], :]).then_inc(f_dev, 1)

            def softplus_correction():
                dve.wait_ge(a_e, a * 2 + 2)
                v.tensor_scalar(lnw, e_neg[:], 1.0, None, ALU.add).then_inc(a_corr, 1)
                dve.wait_ge(a_corr, a * 2 + 1)
                v.scalar_tensor_tensor(e_neg[:], lnw, -1.0, e_neg[:], ALU.add, ALU.subtract).then_inc(a_corr, 1)

            def softplus_end():
                dve.wait_ge(a_ln, a + 1)
                v.tensor_tensor(lnw, lnw, e_neg[:], ALU.subtract).then_inc(a_diff, 1)
                dve.wait_ge(a_diff, a + 1)
                v.scalar_tensor_tensor(delta_next[:], delta_next[:], 0.0, lnw, ALU.max, ALU.add).then_inc(a_delta, 1)

            def split_bc():
                def own(k):
                    dve.wait_ge(a_bc, a * 6 + k)

                src = ps[0:2 * N, bank_A[JA_BC], :]
                dve.wait_ge(a_job, a * JA + JA)
                v.tensor_copy(BC3_next[0:2 * N, :], src).then_inc(a_bc, 1)
                own(1)
                v.tensor_tensor(split[:, 0, :], src, BC3_next[0:2 * N, :], ALU.subtract).then_inc(a_bc, 1)
                own(2)
                v.tensor_copy(mid16, split[:, 0, :]).then_inc(a_bc, 1)
                own(3)
                v.tensor_tensor(split[:, 1, :], split[:, 0, :], mid16, ALU.subtract).then_inc(a_bc, 1)
                own(4)
                v.tensor_copy(BC3_next[2 * N:4 * N, :], mid16).then_inc(a_bc, 1)
                v.tensor_copy(BC3_next[4 * N:6 * N, :], split[:, 1, :]).then_inc(a_bc, 1)

            def floor_delta():
                dve.wait_ge(a_delta, a + 1)
                for g in range(G):
                    ins = v.tensor_scalar(lnw[:, g, :], delta_next[:, g, :], delta_lo[:, g:g + 1], DELTA_HI, ALU.max, ALU.min)
                ins.then_inc(a_floor, 1)

            def newton():
                dve.wait_ge(a_rd, a * 2 + 2)
                v.tensor_tensor(lnw, lnw, nrd_next[:], ALU.mult).then_inc(a_newton, 1)
                dve.wait_ge(a_newton, a * 2 + 1)
                v.scalar_tensor_tensor(nrd_next[:], lnw, -2.0, nrd_next[:], ALU.add, ALU.mult).then_inc(a_newton, 1)

            def ratio(n):
                c = it * N + n
                if n == 0:
                    dve.wait_ge(nrd_moved, it + 1)
                dve.wait_ge(inv_steps, 3 * c + 3)
                for g in range(G):
                    ins = v.scalar_tensor_tensor(inv[:, n % 2, g, :], nrd[:, g, :], inv_kappa[:, n, g:g + 1],
                                                 inv[:, n % 2, g, :], ALU.add, ALU.mult)
                ins.then_inc(ratio_done, 1)

            def expm1(n):
                dve.wait_ge(exp_done, it * N + n + 1)
                v.scalar_tensor_tensor(th[:, n % 2], abar[:, n % 2], 1.0, th[:, n % 2], ALU.add, ALU.mult).then_inc(em1_done, 1)

            def finish_block():
                dve.wait_ge(f_dev, f * DEV_F + 1 + DEV_F)
                v.tensor_tensor(xn[:], xn[:], rows[:, 1, :].unsqueeze(1).broadcast_to([P, TPB, D]), ALU.mult).then_inc(f_fin, 1)
                dve.wait_ge(f_fin, f + 1)
                v.tensor_tensor(xn[:], xn[:], x1[:], ALU.add).then_inc(f_out, 1)

            def background(slot, place):
                if F:
                    if slot == 0 and place == 2:
                        normalize_f1()
                    if slot == 2 and place == 0:
                        gated()
                    if slot == 2 and place in (2, 3, 4, 5):
                        take_out(place - 2)
                    if slot == 3 and place == 0:
                        resid_after()
                    if slot == 4 and place == 0:
                        normalize_f2()
                    if slot == 6 and place == 1:
                        top_two()
                    if slot == 8 and place == 1:
                        take_gT()
                    if slot >= SLOT_W2 and place in (2, 3):
                        w2_sum(slot - SLOT_W2, place - 2)
                    if slot >= SLOT_W2 and place == 4:
                        w2_sum(slot - SLOT_W2, 2)
                        w2_sum(slot - SLOT_W2, 3)
                    if slot == N - 1 and place == 5:
                        finish_block()
                if A:
                    if slot == 0 and place == 5:
                        stats_A()
                    if slot == 2 and place == 0:
                        norm_A()
                    if slot == 4 and place == 5:
                        conv()
                    if slot == 8 and place == 5:
                        softplus_correction()
                    if slot == 10 and place == 5:
                        softplus_end()
                    if slot == 11 and place == 1:
                        split_bc()
                    if slot == 11 and place == 2:
                        floor_delta()
                    if slot == 13 and place == 1:
                        newton()

            for n in range(N):
                p = n % 2
                c = it * N + n
                background(n, 0)
                if scan:
                    if n == 0:
                        ratio(n)
                    expm1(n)
                    dve.wait_ge(ratio_done, c + 1)
                    dve.wait_ge(em1_done, c + 1)
                    v.tensor_tensor(th[:, p], inv[:, p], th[:, p], ALU.mult).then_inc(factor_done, 1)
                background(n, 1)
                if scan:
                    dve.wait_ge(B_ready, c + 1)
                    dve.wait_ge(factor_done, c + 1)
                    if n == 1:
                        dve.wait_ge(u_moved, it + 1)
                    uu = u_next if n == 0 else u
                    for g in range(G):
                        ins = v.scalar_tensor_tensor(inv[:, p, g, :], uu[:, g, :], coef[:, n, g:g + 1],
                                                     ps[:, B_BANK, :], ALU.mult, ALU.mult)
                    ins.then_inc(w_done, 1)
                background(n, 2)
                if scan:
                    dve.wait_ge(w_done, c + 1)
                    v.tensor_tensor(inv[:, p], inv[:, p], th[:, p], ALU.mult).then_inc(bu_done, 1)
                background(n, 3)
                if scan:
                    ge(dve, y_summed, c)
                    ge(dve, carry_done, it * (N + 1))
                    dve.wait_ge(bu_done, c + 1)
                    for g in range(G):
                        ins = v.tensor_tensor_scan(hs[:, g, :], abar[:, p, g, :], inv[:, p, g, :], carry[:, n, g:g + 1],
                                                   ALU.mult, ALU.add)
                    ins.then_inc(scan_done, 1)
                background(n, 4)
                if scan:
                    dve.wait_ge(scan_done, c + 1)
                    v.tensor_copy(carry[:, n, :], hs[:, :, T - 1]).then_inc(carry_done, 1)
                    if n + 1 < N:
                        ratio(n + 1)
                if scan:
                    dve.wait_ge(C_ready, c + 1)
                    dve.wait_ge(carry_done, it * (N + 1) + n + 1)
                    v.tensor_tensor(hs[:], hs[:], ps[:, C_BANK:C_BANK + 1, :].broadcast_to([P, G, T]), ALU.mult).then_inc(hC_done, 1)
                background(n, 5)
            if scan and A:
                dve.wait_ge(carry_done, it * (N + 1) + N)
                v.tensor_scalar(carry[:], carry[:], keep_lim[:, 0, bass.ds(a, 1)], keep_lim[:, 1, bass.ds(a, 1)],
                                ALU.min, ALU.max).then_inc(carry_done, 1)
            if A:
                ge(dve, C_ready, it * N + N)
                dve.wait_ge(a_bc, a * 6 + 6)
                v.tensor_copy(BC3[:], BC3_next[:]).then_inc(bc_moved, 1)

        plans = {key: plan_banks(*key)[0] for key in ((True, True), (True, False), (False, True))}
        bank_A, bank_F = {}, {}

        def use(A, F):
            plan = plans[(A, F)]
            bank_A.clear()
            bank_F.clear()
            for (kind, no), (bank, _) in plan.items():
                (bank_A if kind == "A" else bank_F)[no] = bank
            return plan

        def steps(emit, loop):
            emit(-1, False, True, False, False)
            emit(0, True, True, False, False)
            with loop(1, NBLK - 1) as it:
                emit(it, True, True, True, True)
            emit(NBLK - 1, True, False, True, True)
            emit(NBLK, False, False, True, True)

        with nc.Block() as block:
            @block.sync
            def _(sp):
                steps(lambda it, scan, A, F, prev: sync_block(sp, it, scan, A, F), sp.Fori)
                sp.wait_ge(f_st, 16 * NBLK + 1)

            @block.scalar
            def _(act):
                def emit(it, scan, A, F, prev):
                    use(A, F)
                    act_block(act, it, scan, A, F, prev)
                steps(emit, act.Fori)

            @block.tensor
            def _(pe):
                def emit(it, scan, A, F, prev):
                    pe_block(pe, it, scan, A, F, prev, use(A, F))
                steps(emit, pe.Fori)

            @block.vector
            def _(dve):
                nc.vector.memset(gsum[:, 0:1], 0.0).then_inc(f_out, 1)
                nc.vector.memset(gsum[:, 1:2], 0.0).then_inc(f_st, 1)
                nc.vector.memset(gsum[:, 2:3], 0.0).then_inc(f_dev, 1)

                def emit(it, scan, A, F, prev):
                    use(A, F)
                    dve_block(dve, it, scan, A, F)
                steps(emit, dve.Fori)


def kernel(**inputs):
    import numpy as _np
    import concourse.bacc as _bacc
    from concourse import mybir as _mybir
    from concourse.bass_utils import run_bass_kernel_spmd as _run

    a = {k: _np.asarray(v) for k, v in inputs.items()}
    NB, L, D = a["L0_attn_x"].shape
    N = a["L0_attn_A_log"].shape[1]
    E, _, H = a["L0_ffn_W1"].shape
    c = _np.ascontiguousarray
    laid = {
        "x": a["L0_attn_x"],
        "W_in": a["L0_attn_W_in"],
        "conv_w": a["L0_attn_conv_w"][:, 0, :],
        "W_BC": _np.concatenate([a["L0_attn_W_B"], a["L0_attn_W_C"]], axis=1),
        "W_deltaT": a["L0_attn_W_delta"].T,
        "delta_base": a["L0_attn_delta_base"],
        "W_tau": a["L0_attn_W_tau"],
        "A_log": a["L0_attn_A_log"],
        "W_out": a["L0_attn_W_out"],
        "gate_W": a["L0_ffn_gate_W"],
        "W1": _np.concatenate([a["L0_ffn_W1"].transpose(1, 0, 2).reshape(D, E * H), a["L0_ffn_Ws1"]], axis=1),
        "b1": _np.concatenate([a["L0_ffn_b1"].reshape(E * H), a["L0_ffn_bs1"]]),
        "W2": _np.concatenate([a["L0_ffn_W2"].reshape(E * H, D), a["L0_ffn_Ws2"]], axis=0),
        "b2": _np.concatenate([a["L0_ffn_b2"], a["L0_ffn_bs2"][None, :]], axis=0),
        "route_scale": a["L0_ffn_route_scale"].reshape(1),
        "cT": a["L0_c"].T,
        "wmod": a["L0_wmod"],
        "ident": _np.eye(128, dtype=_np.float32),
        "onehot": _np.tile(_np.eye(2 * N, dtype=_np.float32), (3, 1)).astype(_mybir.dt.np(_mybir.dt.bfloat16)),
        "earlier": _np.tril(_np.ones((E, E), _np.float32), -1).reshape(E * E),
        "keep": _np.array([s * (0.0 if i % (L // 512) == 0 else float(_np.finfo(_np.float32).max)) for s in (1, -1) for i in range(NB * L // 512)],
                          _np.float32),
    }
    nc = _bacc.Bacc("TRN2", target_bir_lowering=False, num_devices=1)
    arrays, args = {}, []
    for name, arr in laid.items():
        arr = c(arr)
        arrays[f"in_{name}"] = arr
        args.append(nc.dram_tensor(f"in_{name}", arr.shape, _mybir.dt.from_np(arr.dtype), kind="ExternalInput").ap())
    args.append(nc.dram_tensor("out_0", a["L0_attn_x"].shape, _mybir.dt.float32, kind="ExternalOutput").ap())
    adaln_mamba_moe(nc, *args)
    r = _run(nc, [arrays], core_ids=[0])
    return r.results[0]["out_0"]
```
